# Optimizing a Trainium2 kernel written in Bass

```python
import numpy as np
import jax
import jax.numpy as jnp

def _softmax(x, axis=-1):
    return jax.nn.softmax(x, axis=axis)

def _gelu(x):
    return jax.nn.gelu(x, approximate=True)

def _silu(x):
    return jax.nn.silu(x)

def _sigmoid(x):
    return jax.nn.sigmoid(x)

def _layernorm(x, axis=-1, eps=1e-05):
    m = jnp.mean(x, axis=axis, keepdims=True)
    v = jnp.var(x, axis=axis, keepdims=True)
    return (x - m) / jnp.sqrt(v + eps)

def _scatter_add(tgt, idx, src, axis=0):
    return tgt.at[idx].add(src)

def _segment_sum(src, seg, n):
    return jax.ops.segment_sum(src, seg, n)
kernel_name = 'mk_cond_resid_d2_seqx_r2_2ab1ba'

def setup_inputs(seed: int=0):
    np.random.seed(seed)
    _w = jnp.asarray

    def _rec_inputs():
        import jax
        import jax.numpy as jnp
        _rk = jax.random.key(seed)
        x = -0.000125 + 0.9999 * jax.random.normal(jax.random.fold_in(_rk, 1), (16, 512, 512), jnp.float32)
        _lenS = 512 - jax.random.randint(jax.random.fold_in(_rk, 7), (16,), 0, max(1, 512 // 4) + 1, jnp.int32)
        _lenS2 = 512 - jax.random.randint(jax.random.fold_in(_rk, 8), (16,), 0, max(1, 512 // 4) + 1, jnp.int32)
        cond_512 = 0.00782532 + 1.00527 * jax.random.normal(jax.random.fold_in(_rk, 11), (16, 256), jnp.float32)
        return (x, cond_512)
    x, cond_512 = _rec_inputs()

    def _L0_cond_setup():
        import jax, jax.numpy as jnp
        import numpy as np
        IN_DIM = 512
        OUT_DIM = 512
        MU_DIM = 256
        K = 30
        key = jax.random.key(seed)
        k1, k2, k3, k4, k5 = jax.random.split(key, 5)
        B, S = (16, 1024)
        x = jax.random.normal(k1, (B, S, IN_DIM), dtype=jnp.float32)
        mu = jax.random.normal(k2, (B, MU_DIM), dtype=jnp.float32)
        W_dec = jax.random.normal(k3, (MU_DIM, (IN_DIM + 1) * K), dtype=jnp.float32) / np.sqrt(MU_DIM)
        b_dec = jax.random.normal(k4, ((IN_DIM + 1) * K,), dtype=jnp.float32) * 0.01
        V = jax.random.normal(k5, (K, OUT_DIM), dtype=jnp.float32) / np.sqrt(K)
        return {'x': x, 'mu': mu, 'W_dec': W_dec, 'b_dec': b_dec, 'V': V}
    _L0_cond_all = _L0_cond_setup()
    _L0_cond_in = {k: v for k, v in _L0_cond_all.items() if k in ('W_dec', 'b_dec', 'V')}
    del _L0_cond_all

    def _L1_cond_setup():
        import jax, jax.numpy as jnp
        import numpy as np
        W_DIM = 256
        CLAMP = 256.0
        key = jax.random.key(seed)
        ks = jax.random.split(key, 6)
        B, L, C = (8, 4096, 512)
        return {'x': jax.random.normal(ks[0], (B, L, C), dtype=jnp.float32), 'w': jax.random.normal(ks[1], (B, W_DIM), dtype=jnp.float32), 'weight': jax.random.normal(ks[2], (C, C), dtype=jnp.float32), 'bias': jax.random.normal(ks[3], (C,), dtype=jnp.float32), 'affine_w': jax.random.normal(ks[4], (C, W_DIM), dtype=jnp.float32), 'affine_b': jnp.ones((C,), dtype=jnp.float32)}
    _L1_cond_all = _L1_cond_setup()
    _L1_cond_in = {k: v for k, v in _L1_cond_all.items() if k in ('weight', 'bias', 'affine_w', 'affine_b')}
    del _L1_cond_all
    return {'x': x, 'cond_512': cond_512, 'L0_cond_W_dec': _L0_cond_in['W_dec'], 'L0_cond_b_dec': _L0_cond_in['b_dec'], 'L0_cond_V': _L0_cond_in['V'], 'L1_cond_weight': _L1_cond_in['weight'], 'L1_cond_bias': _L1_cond_in['bias'], 'L1_cond_affine_w': _L1_cond_in['affine_w'], 'L1_cond_affine_b': _L1_cond_in['affine_b']}

def reference(x, cond_512, L0_cond_W_dec, L0_cond_b_dec, L0_cond_V, L1_cond_weight, L1_cond_bias, L1_cond_affine_w, L1_cond_affine_b):
    import jax
    import jax.numpy as jnp

    def _L0_cond_ref(x, mu, W_dec, b_dec, V):
        import jax, jax.numpy as jnp
        import numpy as np
        IN_DIM = 512
        OUT_DIM = 512
        MU_DIM = 256
        K = 30
        B = mu.shape[0]
        U = (mu @ W_dec + b_dec).reshape(B, IN_DIM + 1, K)
        param = jnp.einsum('bik,kj->bij', U, V)
        weight = param[:, :-1, :]
        bias = param[:, -1, :]
        out = jnp.einsum('bsd,bde->bse', x, weight)
        out = out + bias[:, None, :]
        return out

    def _L1_cond_ref(x, w, weight, bias, affine_w, affine_b):
        import jax, jax.numpy as jnp
        import numpy as np
        W_DIM = 256
        CLAMP = 256.0
        B, L, C = x.shape
        gain = 1.0 / np.sqrt(W_DIM).astype(np.float32)
        styles = w @ (affine_w * gain).T + affine_b
        ws = weight[None, :, :] * styles[:, None, :]
        dcoefs = jax.lax.rsqrt(jnp.sum(ws * ws, axis=2) + 1e-08)
        xm = x * styles[:, None, :]
        y = jnp.einsum('blc,oc->blo', xm, weight)
        y = y * dcoefs[:, None, :]
        y = jnp.clip(y + bias, -CLAMP, CLAMP)
        return y
    x = x + _L0_cond_ref(x, cond_512, L0_cond_W_dec, L0_cond_b_dec, L0_cond_V)
    x = x + _L1_cond_ref(x, cond_512, L1_cond_weight, L1_cond_bias, L1_cond_affine_w, L1_cond_affine_b)
    return x

_drawn_inputs = setup_inputs


def setup_inputs(seed=0):
    import zlib

    import numpy as np

    out = dict(_drawn_inputs(seed))
    spreads = {'L1_cond_affine_b': (1.0, 0.2)}
    factors = {'L0_cond_b_dec': 5.667}
    for name, (base, spread) in spreads.items():
        noise = np.random.default_rng([zlib.crc32(name.encode()), seed]).standard_normal(out[name].shape)
        drawn = base * np.exp(spread * noise) if base else spread * noise
        out[name] = jnp.asarray(drawn.astype(out[name].dtype))
    for name, factor in factors.items():
        out[name] = (out[name] * factor).astype(out[name].dtype)
    return out
```

```python
from contextlib import ExitStack

import concourse.bass as bass
from concourse import mybir

fp32 = mybir.dt.float32
fp32r = mybir.dt.float32r
ALU = mybir.AluOpType
ACT = mybir.ActivationFunctionType

P = 128


def build(nc, x, cond, w_dec, b_dec, v_mat, weight, bias, affine_w, affine_b, out):
    B, S, C = x.shape
    MU = cond.shape[1]
    K = v_mat.shape[0]
    CT, TT, MT = C // P, S // P, MU // P
    GR = P // 4
    CLAMP = 256.0
    EPS = 1e-8
    GAIN = 1.0 / MU ** 0.5
    TILE_COLS = P * K
    CHUNKS = 8
    CHUNK = TILE_COLS // CHUNKS
    DEC_BUFS = 3
    BG = P // CT
    KB = 4
    NT = CT
    TB = 4
    LAG = 2

    ctx = ExitStack()
    with ctx:
        def sb(name, shape, dt=fp32):
            return ctx.enter_context(nc.sbuf_tensor(name, shape, dt))

        def pb(name, shape):
            return ctx.enter_context(nc.psum_tensor(name, shape, fp32))

        def sem(name):
            return ctx.enter_context(nc.semaphore(name))

        ident = sb("ident", [P, P])
        cond_rows = sb("cond_rows", [B, MU])
        vec_rows = sb("vec_rows", [2 * CT, P])
        cond_t = sb("cond_t", [P, MT, BG])
        vec_cols = sb("vec_cols", [P, 2 * CT])
        affb_col = vec_cols[:, 0:CT]
        bias_col = vec_cols[:, CT:2 * CT]
        dec = [sb(f"dec{n}", [P, MT, CT, CHUNK]) for n in range(DEC_BUFS)]
        u_rows = sb("u_rows", [P, TILE_COLS])
        dec_last = sb("dec_last", [P, MT, K])
        dec_last4 = sb("dec_last4", [P, MT, 4, GR])
        bdec_col = sb("bdec_col", [P, CT, K])
        bdec_last = sb("bdec_last", [P, 1])
        u_all = sb("u_all", [P, B, CT, GR])
        u_b = [sb(f"u_b{n}", [P, CT, GR]) for n in range(2)]
        u_stat = [sb(f"u_stat{n}", [P, CT, 4, GR], fp32r) for n in range(2)]
        v_raw = sb("v_raw", [P, C])
        v_stat = sb("v_stat", [P, C], fp32r)
        w_hi = sb("w_hi", [P, CT, C], fp32r)
        w_lo = sb("w_lo", [P, CT, C], fp32r)
        style_sq = sb("style_sq", [P, CT, B])
        var = sb("var", [P, CT, B])
        inv = sb("inv", [P, CT, B])
        newton = sb("newton", [P, CT, B])
        S0, D0, U0, TAB = 0, CT, 2 * CT, 2 * CT + 1
        tab_all = sb("tab_all", [P, B, TAB])
        tab = [sb(f"tab{n}", [P, TAB]) for n in range(2)]
        x_in = [sb(f"x_in{n}", [P, TT, C]) for n in range(2)]
        xt_hi = sb("xt_hi", [P, CT, S], fp32r)
        xt_lo = sb("xt_lo", [P, CT, S], fp32r)
        h_stack = sb("h_stack", [P, S], fp32r)
        xm_hi = [sb(f"xm_hi{n}", [P, CT, S], fp32r) for n in range(2)]
        xm_lo = [sb(f"xm_lo{n}", [P, CT, S], fp32r) for n in range(2)]
        x1 = [sb(f"x1_{n}", [P, CT, S]) for n in range(2)]
        res = [sb(f"res{n}", [P, S]) for n in range(TB)]
        out_sb = [sb(f"out_sb{n}", [P, TT, C]) for n in range(2)]
        weight_rows, w_sq = out_sb
        affine_rows = x1[0][:, :, 0:MU]
        affine_t = x1[1][:, 0:MT, :]

        xt_ps = pb("xt_ps", [P, CT, S])
        h_ps = pb("h_ps", [P, S])
        y_ps = [pb(f"y_ps{n}", [P, S]) for n in range(2)]
        o_ps = pb("o_ps", [P, TT, P])

        cond_loaded = sem("cond_loaded")
        affine_loaded = sem("affine_loaded")
        weight_loaded = sem("weight_loaded")
        vec_loaded = sem("vec_loaded")
        bdec_loaded = sem("bdec_loaded")
        last_loaded = sem("last_loaded")
        v_loaded = sem("v_loaded")
        dec_loaded = [sem(f"dec_loaded{n}") for n in range(DEC_BUFS)]
        x_loaded = [sem(f"x_loaded{n}") for n in range(2)]
        out_stored = [sem(f"out_stored{n}") for n in range(2)]
        zeroed = sem("zeroed")
        ident_ready = sem("ident_ready")
        last_ready = sem("last_ready")
        setup_pe = sem("setup_pe")
        setup_act = sem("setup_act")
        setup_dve = sem("setup_dve")
        u_made = sem("u_made")
        u_in_rows = sem("u_in_rows")
        u_turned = sem("u_turned")
        u_kept = sem("u_kept")
        u_fetched = sem("u_fetched")
        stat_ready = sem("stat_ready")
        xt_done = sem("xt_done")
        xt_hi_done = sem("xt_hi_done")
        xt_lo_done = sem("xt_lo_done")
        h_done = sem("h_done")
        h_hi_done = sem("h_hi_done")
        h_stacked = sem("h_stacked")
        x1_done = sem("x1_done")
        xm_hi_done = sem("xm_hi_done")
        xm_lo_done = sem("xm_lo_done")
        x1_copied = sem("x1_copied")
        y_done = sem("y_done")
        y_scaled = sem("y_scaled")
        clipped = sem("clipped")
        res_ready = sem("res_ready")
        o_done = sem("o_done")
        o_copied = sem("o_copied")

        block = ctx.enter_context(nc.Block())

        x_v = x.rearrange("b (t p) c -> b p t c", p=P)
        out_v = out.rearrange("b (t p) c -> b p t c", p=P)
        dec_v = w_dec.rearrange("(m p) n -> p m n", p=P)
        dec_tiles = dec_v[:, :, 0:C * K].rearrange("p m (t n) -> p m t n", t=CT)

        TURNS = (1, B // 2 - 1)

        def run_steps(eng, step):
            for half in range(2):
                step(0, half, seen=half)
            with eng.Fori(*TURNS) as turn:
                for half in range(2):
                    step(turn, half, seen=2)
            for half in range(2):
                step(B // 2 - 1, half, seen=2, last=half == 1)

        @block.sync
        def _(eng):
            def load_dec(q):
                if q >= DEC_BUFS:
                    eng.wait_ge(u_made, q - DEC_BUFS + 1)
                for m in range(MT):
                    eng.dma_start(dec[q % DEC_BUFS][:, m, :, :], dec_tiles[:, m, :, q * CHUNK:(q + 1) * CHUNK])\
                        .then_inc(dec_loaded[q % DEC_BUFS], 16)

            eng.dma_start(cond_rows[:, :], cond).then_inc(cond_loaded, 16)
            load_dec(0)
            load_dec(1)
            eng.dma_start(affine_rows, affine_w.rearrange("(t p) m -> p t m", p=P)).then_inc(affine_loaded, 16)
            eng.dma_start(weight_rows[:, :, :], weight.rearrange("(t p) c -> p t c", p=P))\
                .then_inc(weight_loaded, 16)
            for q in range(2, CHUNKS):
                load_dec(q)
            eng.dma_start(x_in[0][:, :, :], x_v[0]).then_inc(x_loaded[0], 16)
            eng.dma_start(x_in[1][:, :, :], x_v[1]).then_inc(x_loaded[1], 16)

            def step(turn, half, seen, last=False):
                b = 2 * turn + half
                if not (last or (isinstance(turn, int) and turn == B // 2 - 1)):
                    eng.wait_ge(xt_done, CT * (b + 1))
                    eng.dma_start(x_in[half][:, :, :], x_v[b + 2]).then_inc(x_loaded[half], 16)
                eng.wait_ge(o_copied, NT * (b + 1))
                eng.dma_start(out_v[b], out_sb[half][:, :, :]).then_inc(out_stored[half], 16)

            run_steps(eng, step)
            for half in range(2):
                eng.wait_ge(out_stored[half], 16 * (B // 2))

        @block.scalar
        def _(eng):
            eng.dma_start(vec_rows[0:CT, :], affine_b.rearrange("(t p) -> t p", p=P)).then_inc(vec_loaded, 16)
            eng.dma_start(vec_rows[CT:2 * CT, :], bias.rearrange("(t p) -> t p", p=P)).then_inc(vec_loaded, 16)
            eng.dma_start(dec_last[:, :, :], dec_v[:, :, C * K:(C + 1) * K]).then_inc(last_loaded, 16)
            eng.dma_start(bdec_col[:, :, :], b_dec[0:C * K].rearrange("(t p k) -> p t k", p=P, k=K))\
                .then_inc(bdec_loaded, 16)
            eng.wait_ge(zeroed, 2)
            for g in range(4):
                eng.dma_start(v_raw[g * GR:g * GR + K, :], v_mat).then_inc(v_loaded, 16)
            for g in range(3):
                eng.dma_start(bdec_last[g * GR:g * GR + K, :],
                              b_dec[C * K:(C + 1) * K].rearrange("(k a) -> k a", a=1)).then_inc(bdec_loaded, 16)

            eng.wait_ge(zeroed, 3)
            eng.wait_ge(setup_pe, 1)
            eng.activation(cond_t[:, :, 0:B], h_ps[:, 0:MT * B].rearrange("p (m b) -> p m b", m=MT),
                           ACT.Identity)
            eng.activation(vec_cols[:, :], h_ps[:, MT * B:MT * B + 2 * CT], ACT.Identity)\
                .then_inc(setup_act, 1)
            eng.wait_ge(v_loaded, 16 * 4)
            eng.activation(v_stat[:, :], v_raw[:, :], ACT.Identity).then_inc(setup_act, 1)

            def keep_rows(q):
                eng.wait_ge(u_made, q + 1)
                eng.activation(u_rows[:, q * CHUNK:(q + 1) * CHUNK], y_ps[q % 2][:, 0:CHUNK], ACT.Identity)\
                    .then_inc(u_in_rows, 1)

            keep_rows(0)
            keep_rows(1)
            for m in range(MT):
                eng.wait_ge(setup_pe, 2 + m)
                eng.activation(affine_t[:, m, :], y_ps[m][:, :], ACT.Identity).then_inc(setup_act, 1)
            for c in range(CT):
                eng.wait_ge(setup_pe, 4 + c)
                eng.activation(w_hi[:, c, :], xt_ps[:, c, :], ACT.Identity).then_inc(setup_act, 1)
            for c in range(CT):
                eng.wait_ge(setup_dve, 2 + c)
                eng.activation(w_sq[:, c, :], xt_ps[:, c, :], ACT.Square).then_inc(setup_act, 1)
            keep_rows(2)
            eng.wait_ge(setup_dve, 8)
            eng.activation(inv[:, :, :], var[:, :, :], ACT.Sqrt).then_inc(setup_act, 1)
            for q in range(3, CHUNKS):
                keep_rows(q)

            def split_xt(turn, half):
                b = 2 * turn + half
                for c in range(CT):
                    eng.wait_ge(xt_done, CT * b + c + 1)
                    eng.activation(xt_hi[:, c, :], xt_ps[:, c, :], ACT.Identity).then_inc(xt_hi_done, 1)

            def stack_h(turn, half, seen):
                b = 2 * turn + half
                eng.wait_ge(h_done, b + 1)
                eng.activation(h_stack[:, :], h_ps[:, :], ACT.Identity, bias=tab[half][:, U0:U0 + 1])\
                    .then_inc(h_hi_done, 1)

            def split_x1(turn, half):
                b = 2 * turn + half
                for c in range(CT):
                    eng.wait_ge(x1_done, CT * b + c + 1)
                    eng.activation(xm_hi[half][:, c, :], xt_ps[:, c, :], ACT.Identity,
                                   scale=tab[half][:, S0 + c:S0 + c + 1]).then_inc(xm_hi_done, 1)

            def copy_x1(turn, half, seen):
                b = 2 * turn + half
                eng.wait_ge(xm_lo_done, CT * (b + 1))
                if seen >= 2:
                    eng.wait_ge(res_ready, NT * (b - 1))
                eng.activation(x1[half][:, :, :], xt_ps[:, :, :], ACT.Identity).then_inc(x1_copied, 1)

            def scale_y(turn, half, j, seen):
                n = NT * (2 * turn + half) + j
                eng.wait_ge(y_done, n + 1)
                if seen >= 1:
                    eng.wait_ge(o_done, n - TB + 1)
                eng.activation(res[j][:, :], y_ps[j % 2][:, :], ACT.Identity,
                               bias=bias_col[:, j:j + 1], scale=tab[half][:, D0 + j:D0 + j + 1])\
                    .then_inc(y_scaled, 1)

            split_xt(0, 0)
            eng.wait_ge(stat_ready, 1)
            stack_h(0, 0, 0)
            split_x1(0, 0)
            copy_x1(0, 0, 0)

            def step(turn, half, seen, last=False):
                nxt = (turn + half, 1 - half)
                scale_y(turn, half, 0, seen)
                if not last:
                    split_xt(*nxt)
                scale_y(turn, half, 1, seen)
                if not last:
                    eng.wait_ge(stat_ready, 2 * nxt[0] + nxt[1] + 1)
                    stack_h(*nxt, seen)
                scale_y(turn, half, 2, seen)
                if not last:
                    split_x1(*nxt)
                scale_y(turn, half, 3, seen)
                if not last:
                    copy_x1(*nxt, seen=seen + 1)

            run_steps(eng, step)

        @block.vector
        def _(eng):
            eng.wait_ge(setup_act, 2)
            eng.tensor_tensor(v_stat[GR:2 * GR, :], v_raw[GR:2 * GR, :], v_stat[GR:2 * GR, :].bitcast(fp32),
                              ALU.subtract).then_inc(setup_dve, 1)
            for c in range(CT):
                eng.wait_ge(setup_act, 5 + c)
                eng.tensor_tensor(w_lo[:, c, :], xt_ps[:, c, :], w_hi[:, c, :].bitcast(fp32),
                                  ALU.subtract).then_inc(setup_dve, 1)
            eng.wait_ge(setup_act, 2)
            eng.wait_ge(setup_pe, 8)
            s_view = tab_all[:, :, S0:S0 + CT].rearrange("p b c -> p c b")
            eng.scalar_tensor_tensor(s_view, o_ps[:, 0, 0:CT * B].rearrange("p (c b) -> p c b", c=CT), GAIN,
                                     affb_col.unsqueeze(2).broadcast_to([P, CT, B]),
                                     ALU.mult, ALU.add).then_inc(setup_dve, 1)
            eng.wait_ge(setup_dve, 6)
            eng.tensor_tensor(style_sq[:, :, :], s_view, s_view, ALU.mult).then_inc(setup_dve, 1)
            eng.wait_ge(setup_pe, 9)
            eng.tensor_scalar(var[:, :, :], o_ps[:, 1, 0:CT * B].rearrange("p (c b) -> p c b", c=CT), EPS, None,
                              ALU.add).then_inc(setup_dve, 1)
            eng.wait_ge(setup_act, 13)
            eng.reciprocal(inv[:, :, :], inv[:, :, :]).then_inc(setup_dve, 1)
            eng.wait_ge(setup_dve, 9)
            eng.tensor_tensor(newton[:, :, :], inv[:, :, :], inv[:, :, :], ALU.mult).then_inc(setup_dve, 1)
            eng.wait_ge(setup_dve, 10)
            eng.tensor_tensor(newton[:, :, :], newton[:, :, :], var[:, :, :], ALU.mult).then_inc(setup_dve, 1)
            eng.wait_ge(setup_dve, 11)
            eng.tensor_scalar(newton[:, :, :], newton[:, :, :], -0.5, 1.5, ALU.mult, ALU.add)\
                .then_inc(setup_dve, 1)
            eng.wait_ge(setup_dve, 12)
            eng.tensor_tensor(tab_all[:, :, D0:D0 + CT].rearrange("p b c -> p c b"), inv[:, :, :],
                              newton[:, :, :], ALU.mult).then_inc(setup_dve, 1)
            eng.wait_ge(setup_pe, 10)
            eng.wait_ge(bdec_loaded, 16 * 4)
            eng.tensor_scalar(tab_all[:, :, U0:U0 + 1], h_ps[:, 0:B].unsqueeze(2), bdec_last[:, 0:1], None,
                              ALU.add).then_inc(setup_dve, 1)
            eng.wait_ge(zeroed, 4)
            for n, k0 in enumerate(range(0, K, KB)):
                ranks = min(KB, K - k0)
                eng.wait_ge(u_turned, n + 1)
                for t in range(CT):
                    last = eng.tensor_tensor(
                        u_all[:, :, t, k0:k0 + ranks].rearrange("p b k -> p k b"),
                        y_ps[n % 2][:, 0:ranks * P].rearrange("p (k t b) -> p k t b", k=ranks, t=CT)[:, :, t, 0:B],
                        bdec_col[:, t, k0:k0 + ranks].unsqueeze(2).broadcast_to([P, ranks, B]), ALU.add)
                last.then_inc(u_kept, 1)

            def split_xt(turn, half):
                b = 2 * turn + half
                for c in range(CT):
                    eng.wait_ge(xt_hi_done, CT * b + c + 1)
                    eng.tensor_tensor(xt_lo[:, c, :], xt_ps[:, c, :], xt_hi[:, c, :].bitcast(fp32),
                                      ALU.subtract).then_inc(xt_lo_done, 1)

            def stack_h(turn, half):
                b = 2 * turn + half
                lo = slice(2 * GR, 3 * GR)
                eng.wait_ge(h_hi_done, b + 1)
                eng.scalar_tensor_tensor(h_stack[lo, :], h_ps[lo, :], tab[half][lo, U0:U0 + 1],
                                         h_stack[lo, :].bitcast(fp32), ALU.add, ALU.subtract)\
                    .then_inc(h_stacked, 1)

            def split_x1(turn, half):
                b = 2 * turn + half
                for c in range(CT):
                    eng.wait_ge(xm_hi_done, CT * b + c + 1)
                    eng.scalar_tensor_tensor(xm_lo[half][:, c, :], xt_ps[:, c, :], tab[half][:, S0 + c:S0 + c + 1],
                                             xm_hi[half][:, c, :].bitcast(fp32), ALU.mult, ALU.subtract)\
                        .then_inc(xm_lo_done, 1)

            def copy_out(turn, half, j, seen):
                b = 2 * turn + half
                if j == 0 and seen >= 2:
                    eng.wait_ge(out_stored[half], 16 * turn)
                eng.wait_ge(o_done, NT * b + j + 1)
                eng.tensor_copy(out_sb[half][:, :, j * P:(j + 1) * P], o_ps[:, :, :]).then_inc(o_copied, 1)

            def clip(turn, half, j):
                eng.wait_ge(y_scaled, NT * (2 * turn + half) + j + 1)
                eng.tensor_scalar(res[j][:, :], res[j][:, :], CLAMP, -CLAMP, ALU.min, ALU.max)\
                    .then_inc(clipped, 1)

            split_xt(0, 0)
            stack_h(0, 0)
            split_x1(0, 0)

            def step(turn, half, seen, last=False):
                nxt, prev = (turn + half, 1 - half), (turn + half - 1, 1 - half)
                if not last:
                    split_xt(*nxt)
                if seen >= 1:
                    copy_out(*prev, 2, seen - 1)
                clip(turn, half, 0)
                if not last:
                    stack_h(*nxt)
                if seen >= 1:
                    copy_out(*prev, 3, seen - 1)
                clip(turn, half, 1)
                clip(turn, half, 2)
                copy_out(turn, half, 0, seen)
                if not last:
                    split_x1(*nxt)
                clip(turn, half, 3)
                copy_out(turn, half, 1, seen)
                if last:
                    copy_out(turn, half, 2, seen)
                    copy_out(turn, half, 3, seen)

            run_steps(eng, step)

        @block.gpsimd
        def _(eng):
            eng.memset(v_raw[:, :], 0.0).then_inc(zeroed, 1)
            eng.memset(bdec_last[:, :], 0.0).then_inc(zeroed, 1)
            eng.memset(cond_t[:, :, :], 0.0).then_inc(zeroed, 1)
            eng.memset(ident[:, :], 0.0).then_inc(ident_ready, 1)
            eng.wait_ge(ident_ready, 1)
            eng.affine_select(out=ident[:, :], in_=ident[:, :], compare_op=ALU.not_equal, fill=1.0,
                              base=0, pattern=[[-1, P]], channel_multiplier=1).then_inc(ident_ready, 1)
            eng.memset(u_all[:, :, :, :], 0.0).then_inc(zeroed, 1)
            eng.memset(dec_last4[:, :, :, :], 0.0).then_inc(last_ready, 1)
            eng.wait_ge(last_ready, 1)
            eng.wait_ge(last_loaded, 16)
            eng.tensor_copy(dec_last4[:, :, 0:3, 0:K],
                            dec_last[:, :, :].unsqueeze(2).broadcast_to([P, MT, 3, K])).then_inc(last_ready, 1)

            def prepare(turn, half):
                b = 2 * turn + half
                eng.tensor_copy(u_b[half][:, :, :], u_all[:, b, :, :]).then_inc(u_fetched, 1)
                eng.tensor_copy(u_stat[half][:, :, 0:3, :],
                                u_all[:, b, :, :].unsqueeze(2).broadcast_to([P, CT, 3, GR])).then_inc(u_fetched, 1)
                eng.tensor_copy(tab[half][:, :], tab_all[:, b, :])
                eng.wait_ge(u_fetched, 2 * (b + 1))
                eng.tensor_tensor(u_stat[half][:, :, 3, :], u_b[half][:, :, :], u_stat[half][:, :, 0, :].bitcast(fp32),
                                  ALU.subtract).then_inc(stat_ready, 1)

            eng.wait_ge(u_kept, -(-K // KB))
            eng.wait_ge(setup_dve, 14)
            prepare(0, 0)
            prepare(0, 1)

            def step(turn, half, seen, last=False):
                b = 2 * turn + half
                for j in range(NT):
                    n = NT * b + j
                    if j == 0:
                        eng.wait_ge(x1_copied, b + 1)
                    eng.wait_ge(clipped, n + 1)
                    eng.tensor_tensor(res[j][:, :], res[j][:, :], x1[half][:, j, :], ALU.add)\
                        .then_inc(res_ready, 1)
                if not (isinstance(turn, int) and turn == B // 2 - 1):
                    prepare(turn + 1, half)

            run_steps(eng, step)

        @block.tensor
        def _(eng):
            eng.wait_ge(ident_ready, 2)
            eng.wait_ge(cond_loaded, 16)
            for m in range(MT):
                eng.transpose(h_ps[:, m * B:(m + 1) * B], cond_rows[:, m * P:(m + 1) * P], ident[0:B, 0:B])
            eng.wait_ge(vec_loaded, 32)
            eng.transpose(h_ps[:, MT * B:MT * B + 2 * CT], vec_rows[:, :], ident[0:2 * CT, 0:2 * CT])\
                .then_inc(setup_pe, 1)
            def make_u(q):
                eng.wait_ge(dec_loaded[q % DEC_BUFS], 16 * MT * (q // DEC_BUFS + 1))
                for m in range(MT):
                    for t in range(CT):
                        last = eng.matmul(y_ps[q % 2][t * BG:(t + 1) * BG, 0:CHUNK], cond_t[:, m, :],
                                          dec[q % DEC_BUFS][:, m, t, :], start=m == 0, stop=m == MT - 1,
                                          tile_position=(0, t * BG))
                last.then_inc(u_made, 1)

            eng.wait_ge(setup_act, 1)
            make_u(0)
            make_u(1)
            eng.wait_ge(affine_loaded, 16)
            for m in range(MT):
                eng.wait_ge(u_in_rows, m + 1)
                for c in range(CT):
                    last = eng.transpose(y_ps[m][:, c * P:(c + 1) * P], affine_rows[:, c, m * P:(m + 1) * P],
                                         ident[:, :])
                last.then_inc(setup_pe, 1)
            eng.wait_ge(weight_loaded, 16)
            for c in range(CT):
                for o in range(CT):
                    last = eng.transpose(xt_ps[:, c, o * P:(o + 1) * P], weight_rows[:, o, c * P:(c + 1) * P],
                                         ident[:, :])
                last.then_inc(setup_pe, 1)
            eng.wait_ge(setup_act, 4)
            for c in range(CT):
                for m in range(MT):
                    last = eng.matmul(o_ps[:, 0, c * B:(c + 1) * B], affine_t[:, m, c * P:(c + 1) * P],
                                      cond_t[:, m, 0:B], start=m == 0, stop=m == MT - 1)
            last.then_inc(setup_pe, 1)
            make_u(2)
            eng.wait_ge(setup_act, 12)
            eng.wait_ge(setup_dve, 7)
            for o in range(CT):
                for c in range(CT):
                    last = eng.matmul(o_ps[:, 1, o * B:(o + 1) * B], w_sq[:, c, o * P:(o + 1) * P],
                                      style_sq[:, c, :], start=c == 0, stop=c == CT - 1)
            last.then_inc(setup_pe, 1)
            eng.wait_ge(last_ready, 2)
            for m in range(MT):
                last = eng.matmul(h_ps[:, 0:B], dec_last4[:, m, :, :].rearrange("p g k -> p (g k)"),
                                  cond_t[:, m, 0:B], start=m == 0, stop=m == MT - 1)
            last.then_inc(setup_pe, 1)
            for q in range(3, CHUNKS):
                eng.wait_ge(u_in_rows, q - 1)
                make_u(q)
            eng.wait_ge(u_in_rows, CHUNKS)
            for n, k0 in enumerate(range(0, K, KB)):
                if n >= 2:
                    eng.wait_ge(u_kept, n - 1)
                for k in range(k0, min(k0 + KB, K)):
                    last = eng.transpose(y_ps[n % 2][:, (k - k0) * P:(k - k0 + 1) * P],
                                         u_rows[:, k:k + (P - 1) * K + 1:K], ident[:, :])
                last.then_inc(u_turned, 1)

            def transpose_x(turn, half, first=False):
                b = 2 * turn + half
                eng.wait_ge(x_loaded[half], 16 * (turn + 1))
                if not first:
                    eng.wait_ge(x1_copied, b)
                for c in range(CT):
                    for t in range(TT):
                        last = eng.matmul(xt_ps[:, c, t * P:(t + 1) * P], x_in[half][:, t, c * P:(c + 1) * P],
                                          ident[:, :], is_transpose=True, start=t == 0, stop=False,
                                          skip_group_check=True)
                    last.then_inc(xt_done, 1)

            def product_h(turn, half):
                b = 2 * turn + half
                eng.wait_ge(stat_ready, b + 1)
                for c in range(CT):
                    u_c = u_stat[half][:, c, :, :].rearrange("p g k -> p (g k)")
                    for part, x_part, parted in ((0, xt_hi, xt_hi_done), (1, xt_lo, xt_lo_done)):
                        eng.wait_ge(parted, CT * b + c + 1)
                        last = eng.matmul(h_ps[:, :], u_c, x_part[:, c, :], start=c == 0 and part == 0,
                                          stop=c == CT - 1 and part == 1)
                last.then_inc(h_done, 1)

            def add_rank(turn, half):
                b = 2 * turn + half
                eng.wait_ge(h_stacked, b + 1)
                for c in range(CT):
                    eng.matmul(xt_ps[:, c, :], v_stat[:, c * P:(c + 1) * P], h_stack[:, :], start=False,
                               stop=True, skip_group_check=True).then_inc(x1_done, 1)

            def main_tile(turn, half, j, seen):
                b = 2 * turn + half
                n = NT * b + j
                if seen >= 1 or j >= 2:
                    eng.wait_ge(y_scaled, n - 1)
                cols = slice(j * P, (j + 1) * P)
                for c in range(CT):
                    if j == 0:
                        eng.wait_ge(xm_lo_done, CT * b + c + 1)
                    eng.matmul(y_ps[j % 2][:, :], w_hi[:, c, cols], xm_hi[half][:, c, :], start=c == 0, stop=False)
                    eng.matmul(y_ps[j % 2][:, :], w_hi[:, c, cols], xm_lo[half][:, c, :], start=False, stop=False)
                    last = eng.matmul(y_ps[j % 2][:, :], w_lo[:, c, cols], xm_hi[half][:, c, :], start=False,
                                      stop=c == CT - 1)
                last.then_inc(y_done, 1)

            def transpose_out(turn, half, j, seen):
                n = NT * (2 * turn + half) + j
                eng.wait_ge(res_ready, n + 1)
                if seen >= 1 or j >= 1:
                    eng.wait_ge(o_copied, n)
                for t in range(TT):
                    last = eng.transpose(o_ps[:, t, :], res[j][:, t * P:(t + 1) * P], ident[:, :])
                last.then_inc(o_done, 1)

            transpose_x(0, 0, first=True)
            product_h(0, 0)
            add_rank(0, 0)

            def step(turn, half, seen, last=False):
                nxt, prev = (turn + half, 1 - half), (turn + half - 1, 1 - half)
                main_tile(turn, half, 0, seen)
                if not last:
                    transpose_x(*nxt)
                if seen >= 1:
                    transpose_out(*prev, NT - 2, seen)
                main_tile(turn, half, 1, seen)
                if not last:
                    product_h(*nxt)
                if seen >= 1:
                    transpose_out(*prev, NT - 1, seen)
                main_tile(turn, half, 2, seen)
                if not last:
                    add_rank(*nxt)
                transpose_out(turn, half, 0, seen)
                main_tile(turn, half, 3, seen)
                transpose_out(turn, half, 1, seen)
                if last:
                    transpose_out(turn, half, 2, seen)
                    transpose_out(turn, half, 3, seen)

            run_steps(eng, step)


_INS = ["x", "cond_512", "L0_cond_W_dec", "L0_cond_b_dec", "L0_cond_V", "L1_cond_weight", "L1_cond_bias",
        "L1_cond_affine_w", "L1_cond_affine_b"]


def kernel(**inputs):
    import numpy as _np
    import concourse.bacc as _bacc
    from concourse import mybir as _mybir
    from concourse.bass_utils import run_bass_kernel_spmd as _run

    nc = _bacc.Bacc("TRN2", target_bir_lowering=False, num_devices=1)
    arrays, args = {}, []
    for name in _INS:
        a = _np.ascontiguousarray(inputs[name])
        arrays[f"in_{name}_dram"] = a
        args.append(nc.dram_tensor(f"in_{name}_dram", a.shape, _mybir.dt.from_np(a.dtype), kind="ExternalInput").ap())
    shape = tuple(inputs["x"].shape)
    args.append(nc.dram_tensor("out_0_dram", shape, _mybir.dt.float32, kind="ExternalOutput").ap())
    build(nc, *args)
    r = _run(nc, [arrays], core_ids=[0])
    return r.results[0]["out_0_dram"]
```

```python
from contextlib import ExitStack

import concourse.bass as bass
from concourse import mybir

fp32 = mybir.dt.float32
fp32r = mybir.dt.float32r
ALU = mybir.AluOpType
ACT = mybir.ActivationFunctionType

P = 128


def build(nc, x, cond, w_dec, b_dec, v_mat, weight, bias, affine_w, affine_b, out):
    B, S, C = x.shape
    MU = cond.shape[1]
    K = v_mat.shape[0]
    CT, TT, MT = C // P, S // P, MU // P
    GR = P // 4
    CLAMP = 256.0
    EPS = 1e-8
    GAIN = 1.0 / MU ** 0.5
    TILE_COLS = P * K
    CHUNKS = 8
    CHUNK = TILE_COLS // CHUNKS
    DEC_BUFS = 3
    BG = P // CT
    KB = 4
    U_BANKS = -(-K // KB)
    NT = TT

    ctx = ExitStack()
    with ctx:
        def sb(name, shape, dt=fp32):
            return ctx.enter_context(nc.sbuf_tensor(name, shape, dt))

        def pb(name, shape):
            return ctx.enter_context(nc.psum_tensor(name, shape, fp32))

        def sem(name):
            return ctx.enter_context(nc.semaphore(name))

        ident = sb("ident", [P, P])
        cond_rows = sb("cond_rows", [B, MU])
        affb_rows = sb("affb_rows", [CT, P])
        cond_t = sb("cond_t", [P, MT, BG])
        affb_col = sb("affb_col", [P, CT])
        dec = [sb(f"dec{n}", [P, MT, CT, CHUNK]) for n in range(DEC_BUFS)]
        u_rows = sb("u_rows", [P, TILE_COLS])
        dec_last = sb("dec_last", [P, MT, K])
        dec_last4 = sb("dec_last4", [P, MT, 4, GR])
        bdec_col = sb("bdec_col", [P, CT, K])
        bdec_last = sb("bdec_last", [P, 1])
        u_all = sb("u_all", [P, B, CT, GR])
        u_stat = [sb(f"u_stat{n}", [P, CT, 4, GR], fp32r) for n in range(2)]
        v_raw = sb("v_raw", [P, C])
        v_stat = sb("v_stat", [P, C], fp32r)
        w_hi = sb("w_hi", [P, CT, C], fp32r)
        w_lo = sb("w_lo", [P, CT, C], fp32r)
        style_sq = sb("style_sq", [P, CT, B])
        var = sb("var", [B, C])
        inv = sb("inv", [B, C])
        newton = sb("newton", [B, C])
        d_rows = sb("d_rows", [B, C])
        d_dram = nc.dram_tensor("d_dram", [B, C], fp32, kind="Internal").ap()
        d_all = [sb(f"d_all{n}", [P, C]) for n in range(2)]
        bias_all = sb("bias_all", [P, C])
        S0, U0, TAB = 0, CT, CT + 1
        tab_all = sb("tab_all", [P, B, TAB])
        tab = [sb(f"tab{n}", [P, TAB]) for n in range(2)]
        x_in = [sb(f"x_in{n}", [P, TT, C]) for n in range(2)]
        xt_hi = sb("xt_hi", [P, CT, S], fp32r)
        xt_lo = sb("xt_lo", [P, CT, S], fp32r)
        h_stack = sb("h_stack", [P, S], fp32r)
        xm_hi = [sb(f"xm_hi{n}", [P, CT, S], fp32r) for n in range(2)]
        xm_lo = [sb(f"xm_lo{n}", [P, CT, S], fp32r) for n in range(2)]
        x1 = [sb(f"x1_{n}", [P, TT, C]) for n in range(2)]
        y = sb("y", [P, NT, C])
        weight_rows, w_sq = x1
        affine_rows = y[:, 0:MT, :].rearrange("p a (t m) -> p (a t) m", m=MU)
        affine_t = y[:, MT:2 * MT, :]

        xt_ps = pb("xt_ps", [P, CT, S])
        h_ps = pb("h_ps", [P, S])
        y_ps = [pb(f"y_ps{n}", [P, S]) for n in range(2)]
        r_ps = pb("r_ps", [P, C])
        turn_ps = (*y_ps, r_ps)
        rank_ps = (r_ps, h_ps)

        cond_loaded = sem("cond_loaded")
        affine_loaded = sem("affine_loaded")
        weight_loaded = sem("weight_loaded")
        affb_loaded = sem("affb_loaded")
        bias_loaded = sem("bias_loaded")
        d_stored = sem("d_stored")
        d_loaded = [sem(f"d_loaded{n}") for n in range(2)]
        bdec_loaded = sem("bdec_loaded")
        last_loaded = sem("last_loaded")
        v_loaded = sem("v_loaded")
        dec_loaded = [sem(f"dec_loaded{n}") for n in range(DEC_BUFS)]
        x_loaded = [sem(f"x_loaded{n}") for n in range(2)]
        out_stored = [sem(f"out_stored{n}") for n in range(2)]
        zeroed = sem("zeroed")
        ident_ready = sem("ident_ready")
        last_ready = sem("last_ready")
        setup_pe = sem("setup_pe")
        setup_act = sem("setup_act")
        setup_dve = sem("setup_dve")
        u_made = sem("u_made")
        u_in_rows = sem("u_in_rows")
        u_turned = sem("u_turned")
        u_kept = sem("u_kept")
        tab_ready = sem("tab_ready")
        u_hi_done = sem("u_hi_done")
        u_stat_ready = sem("u_stat_ready")
        xt_done = sem("xt_done")
        xt_hi_done = sem("xt_hi_done")
        xt_lo_done = sem("xt_lo_done")
        h_done = sem("h_done")
        h_hi_done = sem("h_hi_done")
        h_stacked = sem("h_stacked")
        x1_done = sem("x1_done")
        xm_hi_done = sem("xm_hi_done")
        xm_lo_done = sem("xm_lo_done")
        rank_done = sem("rank_done")
        x1_made = sem("x1_made")
        y_done = sem("y_done")
        y_scaled = sem("y_scaled")
        biased = sem("biased")
        clipped = sem("clipped")
        out_ready = sem("out_ready")

        block = ctx.enter_context(nc.Block())

        x_v = x.rearrange("b (t p) c -> b p t c", p=P)
        out_v = out.rearrange("b (t p) c -> b p t c", p=P)
        dec_v = w_dec.rearrange("(m p) n -> p m n", p=P)
        dec_tiles = dec_v[:, :, 0:C * K].rearrange("p m (t n) -> p m t n", t=CT)

        TURNS = (1, B // 2 - 1)

        def run_steps(eng, step):
            for half in range(2):
                step(0, half, seen=half)
            with eng.Fori(*TURNS) as turn:
                for half in range(2):
                    step(turn, half, seen=2)
            for half in range(2):
                step(B // 2 - 1, half, seen=2, last=half == 1)

        @block.sync
        def _(eng):
            def load_dec(q):
                if q >= DEC_BUFS:
                    eng.wait_ge(u_made, q - DEC_BUFS + 1)
                for m in range(MT):
                    eng.dma_start(dec[q % DEC_BUFS][:, m, :, :], dec_tiles[:, m, :, q * CHUNK:(q + 1) * CHUNK])\
                        .then_inc(dec_loaded[q % DEC_BUFS], 16)

            eng.dma_start(cond_rows[:, :], cond).then_inc(cond_loaded, 16)
            load_dec(0)
            load_dec(1)
            eng.dma_start(affine_rows, affine_w.rearrange("(t p) m -> p t m", p=P)).then_inc(affine_loaded, 16)
            eng.dma_start(weight_rows[:, :, :], weight.rearrange("(t p) c -> p t c", p=P))\
                .then_inc(weight_loaded, 16)
            for q in range(2, CHUNKS):
                load_dec(q)
            eng.dma_start(x_in[0][:, :, :], x_v[0]).then_inc(x_loaded[0], 16)
            eng.dma_start(x_in[1][:, :, :], x_v[1]).then_inc(x_loaded[1], 16)

            eng.wait_ge(setup_dve, 13)
            eng.dma_start(d_dram, d_rows[:, :]).then_inc(d_stored, 16)
            eng.wait_ge(d_stored, 16)
            for half in range(2):
                eng.dma_start(d_all[half][:, :], d_dram[half].partition_broadcast(P)).then_inc(d_loaded[half], 16)

            def step(turn, half, seen, last=False):
                b = 2 * turn + half
                if not (isinstance(turn, int) and turn == B // 2 - 1):
                    eng.wait_ge(x1_made, NT * (b + 1))
                    eng.dma_start(x_in[half][:, :, :], x_v[b + 2]).then_inc(x_loaded[half], 16)
                    eng.wait_ge(y_scaled, NT * (b + 1))
                    eng.dma_start(d_all[half][:, :], d_dram[b + 2].partition_broadcast(P))\
                        .then_inc(d_loaded[half], 16)
                if not last:
                    eng.wait_ge(out_ready, NT * (b + 1))
                    eng.dma_start(out_v[b], x1[half][:, :, :]).then_inc(out_stored[half], 16)
                else:
                    for t in range(NT):
                        eng.wait_ge(out_ready, NT * b + t + 1)
                        eng.dma_start(out_v[b][:, t, :], x1[half][:, t, :]).then_inc(out_stored[half], 16)

            run_steps(eng, step)
            eng.wait_ge(out_stored[0], 16 * (B // 2))
            eng.wait_ge(out_stored[1], 16 * (B // 2 - 1 + NT))

        @block.scalar
        def _(eng):
            eng.dma_start(affb_rows[:, :], affine_b.rearrange("(t p) -> t p", p=P)).then_inc(affb_loaded, 16)
            eng.dma_start(dec_last[:, :, :], dec_v[:, :, C * K:(C + 1) * K]).then_inc(last_loaded, 16)
            eng.dma_start(bdec_col[:, :, :], b_dec[0:C * K].rearrange("(t p k) -> p t k", p=P, k=K))\
                .then_inc(bdec_loaded, 16)
            eng.wait_ge(zeroed, 2)
            for g in range(4):
                eng.dma_start(v_raw[g * GR:g * GR + K, :], v_mat).then_inc(v_loaded, 16)
            for g in range(3):
                eng.dma_start(bdec_last[g * GR:g * GR + K, :],
                              b_dec[C * K:(C + 1) * K].rearrange("(k a) -> k a", a=1)).then_inc(bdec_loaded, 16)
            eng.dma_start(bias_all[:, :], bias.partition_broadcast(P)).then_inc(bias_loaded, 16)

            eng.wait_ge(zeroed, 3)
            eng.wait_ge(setup_pe, 1)
            eng.activation(cond_t[:, :, 0:B], h_ps[:, 0:MT * B].rearrange("p (m b) -> p m b", m=MT),
                           ACT.Identity)
            eng.activation(affb_col[:, :], h_ps[:, MT * B:MT * B + CT], ACT.Identity)\
                .then_inc(setup_act, 1)
            eng.wait_ge(v_loaded, 16 * 4)
            eng.activation(v_stat[:, :], v_raw[:, :], ACT.Identity).then_inc(setup_act, 1)

            def keep_rows(q):
                eng.wait_ge(u_made, q + 1)
                eng.activation(u_rows[:, q * CHUNK:(q + 1) * CHUNK], y_ps[q % 2][:, 0:CHUNK], ACT.Identity)\
                    .then_inc(u_in_rows, 1)

            keep_rows(0)
            keep_rows(1)
            for m in range(MT):
                eng.wait_ge(setup_pe, 2 + m)
                eng.activation(affine_t[:, m, :], y_ps[m][:, :], ACT.Identity).then_inc(setup_act, 1)
            for c in range(CT):
                eng.wait_ge(setup_pe, 4 + c)
                eng.activation(w_hi[:, c, :], xt_ps[:, c, :], ACT.Identity).then_inc(setup_act, 1)
            for c in range(CT):
                eng.wait_ge(setup_dve, 2 + c)
                eng.activation(w_sq[:, c, :], xt_ps[:, c, :], ACT.Square).then_inc(setup_act, 1)
            keep_rows(2)
            eng.wait_ge(setup_dve, 8)
            eng.activation(inv[:, :], var[:, :], ACT.Sqrt).then_inc(setup_act, 1)
            for q in range(3, CHUNKS):
                keep_rows(q)

            def split_xt(turn, half):
                b = 2 * turn + half
                for c in range(CT):
                    eng.wait_ge(xt_done, CT * b + c + 1)
                    eng.activation(xt_hi[:, c, :], xt_ps[:, c, :], ACT.Identity).then_inc(xt_hi_done, 1)

            def stack_h(turn, half):
                b = 2 * turn + half
                eng.wait_ge(tab_ready, b + 1)
                eng.wait_ge(h_done, b + 1)
                eng.activation(h_stack[:, :], h_ps[:, :], ACT.Identity, bias=tab[half][:, U0:U0 + 1])\
                    .then_inc(h_hi_done, 1)

            def split_x1(turn, half):
                b = 2 * turn + half
                for c in range(CT):
                    eng.wait_ge(x1_done, CT * b + c + 1)
                    eng.activation(xm_hi[half][:, c, :], xt_ps[:, c, :], ACT.Identity,
                                   scale=tab[half][:, S0 + c:S0 + c + 1]).then_inc(xm_hi_done, 1)

            def prepare(turn, half):
                b = 2 * turn + half
                eng.activation(u_stat[half][:, :, 0:3, :],
                               u_all[:, b, :, :].unsqueeze(2).broadcast_to([P, CT, 3, GR]), ACT.Identity)\
                    .then_inc(u_hi_done, 1)
                eng.activation(tab[half][:, :], tab_all[:, b, :], ACT.Identity).then_inc(tab_ready, 1)

            split_xt(0, 0)
            eng.wait_ge(u_kept, U_BANKS)
            eng.wait_ge(setup_dve, 14)
            prepare(0, 0)
            stack_h(0, 0)
            split_x1(0, 0)
            prepare(0, 1)

            def step(turn, half, seen, last=False):
                nxt = (turn + half, 1 - half)
                if last:
                    return
                split_xt(*nxt)
                stack_h(*nxt)
                split_x1(*nxt)
                if not (isinstance(turn, int) and turn == B // 2 - 1):
                    prepare(turn + 1, half)

            run_steps(eng, step)

        @block.vector
        def _(eng):
            eng.wait_ge(setup_act, 2)
            eng.tensor_tensor(v_stat[GR:2 * GR, :], v_raw[GR:2 * GR, :], v_stat[GR:2 * GR, :].bitcast(fp32),
                              ALU.subtract).then_inc(setup_dve, 1)
            for c in range(CT):
                eng.wait_ge(setup_act, 5 + c)
                eng.tensor_tensor(w_lo[:, c, :], xt_ps[:, c, :], w_hi[:, c, :].bitcast(fp32),
                                  ALU.subtract).then_inc(setup_dve, 1)
            eng.wait_ge(setup_act, 2)
            eng.wait_ge(setup_pe, 8)
            s_view = tab_all[:, :, S0:S0 + CT].rearrange("p b c -> p c b")
            eng.scalar_tensor_tensor(s_view, r_ps[:, 0:CT * B].rearrange("p (c b) -> p c b", c=CT), GAIN,
                                     affb_col[:, :].unsqueeze(2).broadcast_to([P, CT, B]),
                                     ALU.mult, ALU.add).then_inc(setup_dve, 1)
            eng.wait_ge(setup_dve, 6)
            eng.tensor_tensor(style_sq[:, :, :], s_view, s_view, ALU.mult).then_inc(setup_dve, 1)
            eng.wait_ge(setup_pe, 9)
            eng.tensor_scalar(var[:, :], r_ps[0:B, :], EPS, None, ALU.add).then_inc(setup_dve, 1)
            eng.wait_ge(setup_act, 13)
            eng.reciprocal(inv[:, :], inv[:, :]).then_inc(setup_dve, 1)
            eng.wait_ge(setup_dve, 9)
            eng.tensor_tensor(newton[:, :], inv[:, :], inv[:, :], ALU.mult).then_inc(setup_dve, 1)
            eng.wait_ge(setup_dve, 10)
            eng.tensor_tensor(newton[:, :], newton[:, :], var[:, :], ALU.mult).then_inc(setup_dve, 1)
            eng.wait_ge(setup_dve, 11)
            eng.tensor_scalar(newton[:, :], newton[:, :], -0.5, 1.5, ALU.mult, ALU.add)\
                .then_inc(setup_dve, 1)
            eng.wait_ge(setup_dve, 12)
            eng.tensor_tensor(d_rows[:, :], inv[:, :], newton[:, :], ALU.mult).then_inc(setup_dve, 1)
            eng.wait_ge(setup_pe, 10)
            eng.wait_ge(bdec_loaded, 16 * 4)
            eng.tensor_scalar(tab_all[:, :, U0:U0 + 1], h_ps[:, 0:B].unsqueeze(2), bdec_last[:, 0:1], None,
                              ALU.add).then_inc(setup_dve, 1)
            eng.wait_ge(zeroed, 4)
            for n, k0 in enumerate(range(0, K, KB)):
                ranks = min(KB, K - k0)
                eng.wait_ge(u_turned, n + 1)
                eng.tensor_tensor(
                    u_all[:, :, :, k0:k0 + ranks].rearrange("p b t k -> p k t b"),
                    turn_ps[n % 3][:, 0:ranks * P].rearrange("p (k t b) -> p k t b", k=ranks, t=CT)[:, :, :, 0:B],
                    bdec_col[:, :, k0:k0 + ranks].rearrange("p t k -> p k t").unsqueeze(3)
                    .broadcast_to([P, ranks, CT, B]), ALU.add).then_inc(u_kept, 1)

            def split_xt(turn, half):
                b = 2 * turn + half
                for c in range(CT):
                    eng.wait_ge(xt_hi_done, CT * b + c + 1)
                    eng.tensor_tensor(xt_lo[:, c, :], xt_ps[:, c, :], xt_hi[:, c, :].bitcast(fp32),
                                      ALU.subtract).then_inc(xt_lo_done, 1)

            def stack_h(turn, half):
                b = 2 * turn + half
                lo = slice(2 * GR, 3 * GR)
                eng.wait_ge(h_hi_done, b + 1)
                eng.scalar_tensor_tensor(h_stack[lo, :], h_ps[lo, :], tab[half][lo, U0:U0 + 1],
                                         h_stack[lo, :].bitcast(fp32), ALU.add, ALU.subtract)\
                    .then_inc(h_stacked, 1)

            def split_x1(turn, half):
                b = 2 * turn + half
                for c in range(CT):
                    eng.wait_ge(xm_hi_done, CT * b + c + 1)
                    eng.scalar_tensor_tensor(xm_lo[half][:, c, :], xt_ps[:, c, :], tab[half][:, S0 + c:S0 + c + 1],
                                             xm_hi[half][:, c, :].bitcast(fp32), ALU.mult, ALU.subtract)\
                        .then_inc(xm_lo_done, 1)

            def u_low(turn, half):
                b = 2 * turn + half
                eng.wait_ge(u_hi_done, b + 1)
                eng.tensor_tensor(u_stat[half][:, :, 3, :], u_all[:, b, :, :], u_stat[half][:, :, 0, :].bitcast(fp32),
                                  ALU.subtract).then_inc(u_stat_ready, 1)

            def make_x1(turn, half, t, seen):
                b = 2 * turn + half
                if t == 0 and seen >= 2:
                    eng.wait_ge(out_stored[half], 16 * turn)
                eng.wait_ge(rank_done, NT * b + t + 1)
                eng.tensor_tensor(x1[half][:, t, :], rank_ps[t % 2][:, :], x_in[half][:, t, :], ALU.add)\
                    .then_inc(x1_made, 1)

            def scale_y(turn, half, t, seen):
                n = NT * (2 * turn + half) + t
                if t == 0:
                    eng.wait_ge(d_loaded[half], 16 * (turn + 1))
                if seen >= 1:
                    eng.wait_ge(out_ready, n - NT + 1)
                eng.wait_ge(y_done, n + 1)
                eng.tensor_tensor(y[:, t, :], y_ps[t % 2][:, :], d_all[half][:, :], ALU.mult).then_inc(y_scaled, 1)

            def clip(turn, half, t):
                eng.wait_ge(biased, NT * (2 * turn + half) + t + 1)
                eng.tensor_scalar(y[:, t, :], y[:, t, :], CLAMP, -CLAMP, ALU.min, ALU.max).then_inc(clipped, 1)

            split_xt(0, 0)
            u_low(0, 0)
            stack_h(0, 0)
            split_x1(0, 0)
            u_low(0, 1)
            make_x1(0, 0, 0, 0)
            make_x1(0, 0, 1, 0)

            def step(turn, half, seen, last=False):
                nxt, prev = (turn + half, 1 - half), (turn + half - 1, 1 - half)
                make_x1(turn, half, 2, seen)
                make_x1(turn, half, 3, seen)
                if seen >= 1:
                    clip(*prev, 3)
                scale_y(turn, half, 0, seen)
                if not last:
                    split_xt(*nxt)
                clip(turn, half, 0)
                scale_y(turn, half, 1, seen)
                if not last:
                    stack_h(*nxt)
                clip(turn, half, 1)
                scale_y(turn, half, 2, seen)
                if not last:
                    split_x1(*nxt)
                    make_x1(*nxt, 0, seen + 1)
                    make_x1(*nxt, 1, seen + 1)
                clip(turn, half, 2)
                scale_y(turn, half, 3, seen)
                if not (isinstance(turn, int) and turn == B // 2 - 1):
                    u_low(turn + 1, half)
                if last:
                    clip(turn, half, 3)

            run_steps(eng, step)

        @block.gpsimd
        def _(eng):
            eng.memset(v_raw[:, :], 0.0).then_inc(zeroed, 1)
            eng.memset(bdec_last[:, :], 0.0).then_inc(zeroed, 1)
            eng.memset(cond_t[:, :, :], 0.0).then_inc(zeroed, 1)
            eng.memset(ident[:, :], 0.0).then_inc(ident_ready, 1)
            eng.wait_ge(ident_ready, 1)
            eng.affine_select(out=ident[:, :], in_=ident[:, :], compare_op=ALU.not_equal, fill=1.0,
                              base=0, pattern=[[-1, P]], channel_multiplier=1).then_inc(ident_ready, 1)
            eng.memset(u_all[:, :, :, :], 0.0).then_inc(zeroed, 1)
            eng.memset(dec_last4[:, :, :, :], 0.0).then_inc(last_ready, 1)
            eng.wait_ge(last_ready, 1)
            eng.wait_ge(last_loaded, 16)
            eng.tensor_copy(dec_last4[:, :, 0:3, 0:K],
                            dec_last[:, :, :].unsqueeze(2).broadcast_to([P, MT, 3, K])).then_inc(last_ready, 1)

            eng.wait_ge(bias_loaded, 16)

            def add_bias(turn, half, t):
                eng.wait_ge(y_scaled, NT * (2 * turn + half) + t + 1)
                eng.tensor_tensor(y[:, t, :], y[:, t, :], bias_all[:, :], ALU.add).then_inc(biased, 1)

            def finish(turn, half, t):
                b = 2 * turn + half
                eng.wait_ge(x1_made, NT * b + t + 1)
                eng.wait_ge(clipped, NT * b + t + 1)
                eng.tensor_tensor(x1[half][:, t, :], x1[half][:, t, :], y[:, t, :], ALU.add).then_inc(out_ready, 1)

            def step(turn, half, seen, last=False):
                add_bias(turn, half, 0)
                if seen >= 1:
                    finish(turn + half - 1, 1 - half, 3)
                for t in range(1, NT):
                    add_bias(turn, half, t)
                    finish(turn, half, t - 1)
                if last:
                    finish(turn, half, NT - 1)

            run_steps(eng, step)

        @block.tensor
        def _(eng):
            eng.wait_ge(ident_ready, 2)
            eng.wait_ge(cond_loaded, 16)
            for m in range(MT):
                eng.transpose(h_ps[:, m * B:(m + 1) * B], cond_rows[:, m * P:(m + 1) * P], ident[0:B, 0:B])
            eng.wait_ge(affb_loaded, 16)
            eng.transpose(h_ps[:, MT * B:MT * B + CT], affb_rows[:, :], ident[0:CT, 0:CT])\
                .then_inc(setup_pe, 1)
            def make_u(q):
                eng.wait_ge(dec_loaded[q % DEC_BUFS], 16 * MT * (q // DEC_BUFS + 1))
                for m in range(MT):
                    for t in range(CT):
                        last = eng.matmul(y_ps[q % 2][t * BG:(t + 1) * BG, 0:CHUNK], cond_t[:, m, :],
                                          dec[q % DEC_BUFS][:, m, t, :], start=m == 0, stop=m == MT - 1,
                                          tile_position=(0, t * BG))
                last.then_inc(u_made, 1)

            eng.wait_ge(setup_act, 1)
            make_u(0)
            make_u(1)
            eng.wait_ge(affine_loaded, 16)
            for m in range(MT):
                eng.wait_ge(u_in_rows, m + 1)
                for c in range(CT):
                    last = eng.transpose(y_ps[m][:, c * P:(c + 1) * P], affine_rows[:, c, m * P:(m + 1) * P],
                                         ident[:, :])
                last.then_inc(setup_pe, 1)
            eng.wait_ge(weight_loaded, 16)
            for c in range(CT):
                for o in range(CT):
                    last = eng.transpose(xt_ps[:, c, o * P:(o + 1) * P], weight_rows[:, o, c * P:(c + 1) * P],
                                         ident[:, :])
                last.then_inc(setup_pe, 1)
            eng.wait_ge(setup_act, 4)
            for c in range(CT):
                for m in range(MT):
                    last = eng.matmul(r_ps[:, c * B:(c + 1) * B], affine_t[:, m, c * P:(c + 1) * P],
                                      cond_t[:, m, 0:B], start=m == 0, stop=m == MT - 1)
            last.then_inc(setup_pe, 1)
            make_u(2)
            eng.wait_ge(setup_act, 12)
            eng.wait_ge(setup_dve, 7)
            for c in range(CT):
                last = eng.matmul(r_ps[0:B, :], style_sq[:, c, :], w_sq[:, c, :], start=c == 0, stop=c == CT - 1)
            last.then_inc(setup_pe, 1)
            eng.wait_ge(last_ready, 2)
            for m in range(MT):
                last = eng.matmul(h_ps[:, 0:B], dec_last4[:, m, :, :].rearrange("p g k -> p (g k)"),
                                  cond_t[:, m, 0:B], start=m == 0, stop=m == MT - 1)
            last.then_inc(setup_pe, 1)
            for q in range(3, CHUNKS):
                eng.wait_ge(u_in_rows, q - 1)
                make_u(q)
            eng.wait_ge(setup_dve, 8)
            eng.wait_ge(u_in_rows, CHUNKS)
            for n, k0 in enumerate(range(0, K, KB)):
                if n >= 3:
                    eng.wait_ge(u_kept, n - 2)
                for k in range(k0, min(k0 + KB, K)):
                    last = eng.transpose(turn_ps[n % 3][:, (k - k0) * P:(k - k0 + 1) * P],
                                         u_rows[:, k:k + (P - 1) * K + 1:K], ident[:, :])
                last.then_inc(u_turned, 1)

            def transpose_x(turn, half):
                eng.wait_ge(x_loaded[half], 16 * (turn + 1))
                for c in range(CT):
                    for t in range(TT):
                        last = eng.matmul(xt_ps[:, c, t * P:(t + 1) * P], x_in[half][:, t, c * P:(c + 1) * P],
                                          ident[:, :], is_transpose=True, start=t == 0, stop=False,
                                          skip_group_check=True)
                    last.then_inc(xt_done, 1)

            def product_h(turn, half, seen):
                b = 2 * turn + half
                eng.wait_ge(u_stat_ready, b + 1)
                if seen >= 1:
                    eng.wait_ge(x1_made, NT * b)
                for c in range(CT):
                    u_c = u_stat[half][:, c, :, :].rearrange("p g k -> p (g k)")
                    for part, x_part, parted in ((0, xt_hi, xt_hi_done), (1, xt_lo, xt_lo_done)):
                        eng.wait_ge(parted, CT * b + c + 1)
                        last = eng.matmul(h_ps[:, :], u_c, x_part[:, c, :], start=c == 0 and part == 0,
                                          stop=c == CT - 1 and part == 1)
                last.then_inc(h_done, 1)

            def add_rank(turn, half):
                b = 2 * turn + half
                eng.wait_ge(h_stacked, b + 1)
                for c in range(CT):
                    eng.matmul(xt_ps[:, c, :], v_stat[:, c * P:(c + 1) * P], h_stack[:, :], start=False,
                               stop=True, skip_group_check=True).then_inc(x1_done, 1)

            def rank_tile(turn, half, t):
                b = 2 * turn + half
                if t >= 2:
                    eng.wait_ge(x1_made, NT * b + t - 1)
                eng.matmul(rank_ps[t % 2][:, :], h_stack[:, t * P:(t + 1) * P], v_stat[:, :], start=True, stop=True)\
                    .then_inc(rank_done, 1)

            def main_tile(turn, half, t, seen):
                b = 2 * turn + half
                n = NT * b + t
                if seen >= 1 or t >= 2:
                    eng.wait_ge(y_scaled, n - 1)
                toks = slice(t * P, (t + 1) * P)
                for c in range(CT):
                    if t == 0:
                        eng.wait_ge(xm_lo_done, CT * b + c + 1)
                    eng.matmul(y_ps[t % 2][:, :], xm_hi[half][:, c, toks], w_hi[:, c, :], start=c == 0, stop=False)
                    eng.matmul(y_ps[t % 2][:, :], xm_hi[half][:, c, toks], w_lo[:, c, :], start=False, stop=False)
                    last = eng.matmul(y_ps[t % 2][:, :], xm_lo[half][:, c, toks], w_hi[:, c, :], start=False,
                                      stop=c == CT - 1)
                    if t == 0 and c in (1, 3):
                        rank_tile(turn, half, 2 + c // 2)
                last.then_inc(y_done, 1)

            transpose_x(0, 0)
            product_h(0, 0, 0)
            add_rank(0, 0)
            rank_tile(0, 0, 0)
            rank_tile(0, 0, 1)

            def step(turn, half, seen, last=False):
                nxt = (turn + half, 1 - half)
                main_tile(turn, half, 0, seen)
                if not last:
                    transpose_x(*nxt)
                main_tile(turn, half, 1, seen)
                if not last:
                    product_h(*nxt, seen + 1)
                main_tile(turn, half, 2, seen)
                if not last:
                    add_rank(*nxt)
                    rank_tile(*nxt, 0)
                    rank_tile(*nxt, 1)
                main_tile(turn, half, 3, seen)

            run_steps(eng, step)


_INS = ["x", "cond_512", "L0_cond_W_dec", "L0_cond_b_dec", "L0_cond_V", "L1_cond_weight", "L1_cond_bias",
        "L1_cond_affine_w", "L1_cond_affine_b"]


def kernel(**inputs):
    import numpy as _np
    import concourse.bacc as _bacc
    from concourse import mybir as _mybir
    from concourse.bass_utils import run_bass_kernel_spmd as _run

    nc = _bacc.Bacc("TRN2", target_bir_lowering=False, num_devices=1)
    arrays, args = {}, []
    for name in _INS:
        a = _np.ascontiguousarray(inputs[name])
        arrays[f"in_{name}_dram"] = a
        args.append(nc.dram_tensor(f"in_{name}_dram", a.shape, _mybir.dt.from_np(a.dtype), kind="ExternalInput").ap())
    shape = tuple(inputs["x"].shape)
    args.append(nc.dram_tensor("out_0_dram", shape, _mybir.dt.float32, kind="ExternalOutput").ap())
    build(nc, *args)
    r = _run(nc, [arrays], core_ids=[0])
    return r.results[0]["out_0_dram"]
```

```python
from contextlib import ExitStack

import concourse.bass as bass
from concourse import mybir

fp32 = mybir.dt.float32
fp32r = mybir.dt.float32r
ALU = mybir.AluOpType
ACT = mybir.ActivationFunctionType

P = 128


def build(nc, x, cond, w_dec, b_dec, v_mat, weight, bias, affine_w, affine_b, out):
    B, S, C = x.shape
    MU = cond.shape[1]
    K = v_mat.shape[0]
    CT, TT, MT = C // P, S // P, MU // P
    GR = P // 4
    CLAMP = 256.0
    EPS = 1e-8
    GAIN = 1.0 / MU ** 0.5
    TILE_COLS = P * K
    CHUNKS = 8
    CHUNK = (P // CHUNKS + 1) * K
    CHUNK_ENDS = [min(q * CHUNK, TILE_COLS) for q in range(CHUNKS + 1)]
    DEC_BUFS = 3
    BG = P // CT
    KB = 4
    U_BANKS = -(-K // KB)
    NT = TT

    HALVES = (slice(0, C // 2), slice(C // 2, C))
    HALF_STEPS = 4

    ctx = ExitStack()
    with ctx:
        def sb(name, shape, dt=fp32):
            return ctx.enter_context(nc.sbuf_tensor(name, shape, dt))

        def pb(name, shape):
            return ctx.enter_context(nc.psum_tensor(name, shape, fp32))

        def sem(name):
            return ctx.enter_context(nc.semaphore(name))

        ident = sb("ident", [P, P])
        cond_rows = sb("cond_rows", [B, MU])
        affb_rows = sb("affb_rows", [CT, P])
        cond_t = sb("cond_t", [P, MT, BG])
        affb_col = sb("affb_col", [P, CT])
        dec = [sb(f"dec{n}", [P, MT, CT, CHUNK]) for n in range(DEC_BUFS)]
        u_rows = sb("u_rows", [P, TILE_COLS])
        dec_last = sb("dec_last", [P, MT, K])
        dec_last4 = sb("dec_last4", [P, MT, 4, GR])
        bdec_col = sb("bdec_col", [P, CT, K])
        bdec_last = sb("bdec_last", [P, 1])
        u_all = sb("u_all", [P, B, CT, GR])
        u_stat = [sb(f"u_stat{n}", [P, CT, 4, GR], fp32r) for n in range(2)]
        v_raw = sb("v_raw", [P, C])
        v_stat = sb("v_stat", [P, C], fp32r)
        vt_hi = sb("vt_hi", [P, CT, P], fp32r)
        vt_lo = sb("vt_lo", [P, CT, P], fp32r)
        va_stat = sb("va_stat", [P, C], fp32r)
        w_hi = sb("w_hi", [P, CT, C], fp32r)
        w_lo = sb("w_lo", [P, CT, C], fp32r)
        style_sq = sb("style_sq", [P, CT, B])
        newton = sb("newton", [B, C])
        d_rows = sb("d_rows", [B, C])
        d_dram = nc.dram_tensor("d_dram", [B, C], fp32, kind="Internal").ap()
        d_all = [sb(f"d_all{n}", [P, C]) for n in range(2)]
        bias_all = sb("bias_all", [P, C])
        var, inv = bias_all[0:B, :], d_all[1][0:B, :]
        S0, U0, TAB = 0, CT, CT + 1
        tab_all = sb("tab_all", [P, B, TAB])
        tab = [sb(f"tab{n}", [P, TAB]) for n in range(2)]
        x_in = [sb(f"x_in{n}", [P, TT, C]) for n in range(2)]
        xt_hi = sb("xt_hi", [P, CT, S], fp32r)
        xt_lo = sb("xt_lo", [P, CT, S], fp32r)
        h_stack = sb("h_stack", [P, S], fp32r)
        xm_hi = [sb(f"xm_hi{n}", [P, CT, S], fp32r) for n in range(2)]
        xm_lo = [sb(f"xm_lo{n}", [P, CT, S], fp32r) for n in range(2)]
        x1 = [sb(f"x1_{n}", [P, TT, C]) for n in range(2)]
        y = sb("y", [P, NT, C])
        weight_rows, w_sq = x_in[0], x1[1]
        va_rows = x1[1][:, 0, :]
        first_h = vt_hi[:, :, :].rearrange("p c k -> p (c k)")
        first_x = x1[0]
        first_rank = dec[0][:, :, :, :].rearrange("p m t n -> p (m t n)")[:, 0:NT * C]\
            .rearrange("p (t c) -> p t c", t=NT)
        early_hi, early_lo = xm_hi[1], xm_lo[1]
        affine_rows = y[:, 0:MT, :].rearrange("p a (t m) -> p (a t) m", m=MU)
        affine_t = y[:, MT:2 * MT, :]

        xt_ps = pb("xt_ps", [P, CT, S])
        h_ps = pb("h_ps", [P, S])
        y_ps = [pb(f"y_ps{n}", [P, S]) for n in range(2)]
        r_ps = pb("r_ps", [P, C])
        turn_ps = (*y_ps, r_ps)
        last_ps = (y_ps[1], r_ps)
        rank_ps = (r_ps, h_ps)

        cond_loaded = sem("cond_loaded")
        affine_loaded = sem("affine_loaded")
        weight_loaded = sem("weight_loaded")
        affb_loaded = sem("affb_loaded")
        bias_loaded = sem("bias_loaded")
        d_stored = sem("d_stored")
        d_loaded = [sem(f"d_loaded{n}") for n in range(2)]
        bdec_loaded = sem("bdec_loaded")
        bdec_last_loaded = sem("bdec_last_loaded")
        last_loaded = sem("last_loaded")
        v_loaded = sem("v_loaded")
        dec_loaded = [[sem(f"dec_loaded{n}_{m}") for m in range(MT)] for n in range(DEC_BUFS)]
        x_loaded = [sem(f"x_loaded{n}") for n in range(2)]
        out_stored = [sem(f"out_stored{n}") for n in range(2)]
        zeroed = sem("zeroed")
        ident_ready = sem("ident_ready")
        last_ready = sem("last_ready")
        setup_pe = sem("setup_pe")
        setup_act = sem("setup_act")
        setup_dve = sem("setup_dve")
        u_made = sem("u_made")
        u_in_rows = sem("u_in_rows")
        u_turned = sem("u_turned")
        u_kept = sem("u_kept")
        tab_ready = sem("tab_ready")
        u_hi_done = sem("u_hi_done")
        u_stat_ready = sem("u_stat_ready")
        xt_done = sem("xt_done")
        xt_hi_done = sem("xt_hi_done")
        xt_lo_done = sem("xt_lo_done")
        h_done = sem("h_done")
        h_hi_done = sem("h_hi_done")
        h_stacked = sem("h_stacked")
        x1_done = sem("x1_done")
        xm_hi_done = sem("xm_hi_done")
        xm_lo_done = sem("xm_lo_done")
        rank_done = sem("rank_done")
        x1_made = sem("x1_made")
        y_done = sem("y_done")
        y_scaled = sem("y_scaled")
        biased = sem("biased")
        clipped = sem("clipped")
        out_ready = sem("out_ready")
        last_y_done = sem("last_y_done")
        last_step = sem("last_step")
        first_rank_kept = sem("first_rank_kept")
        first_y_kept = sem("first_y_kept")
        first_y_done = sem("first_y_done")
        first_y_added = sem("first_y_added")

        block = ctx.enter_context(nc.Block())

        x_v = x.rearrange("b (t p) c -> b p t c", p=P)
        out_v = out.rearrange("b (t p) c -> b p t c", p=P)
        dec_v = w_dec.rearrange("(m p) n -> p m n", p=P)
        dec_tiles = dec_v[:, :, 0:C * K].rearrange("p m (t n) -> p m t n", t=CT)

        TURNS = (1, B // 2 - 1)

        def run_steps(eng, step):
            with eng.Fori(*TURNS) as turn:
                for half in range(2):
                    step(turn, half, seen=2)
            for half in range(2):
                step(B // 2 - 1, half, seen=2, last=half == 1)

        @block.sync
        def _(eng):
            def load_dec(q):
                if q >= DEC_BUFS:
                    eng.wait_ge(u_made, q - DEC_BUFS + 1)
                for m in range(MT):
                    eng.dma_start(dec[q % DEC_BUFS][:, m, :, 0:CHUNK_ENDS[q + 1] - CHUNK_ENDS[q]],
                                  dec_tiles[:, m, :, CHUNK_ENDS[q]:CHUNK_ENDS[q + 1]])\
                        .then_inc(dec_loaded[q % DEC_BUFS][m], 16)

            eng.dma_start(cond_rows[:, :], cond).then_inc(cond_loaded, 16)
            eng.dma_start(affine_rows, affine_w.rearrange("(t p) m -> p t m", p=P)).then_inc(affine_loaded, 16)
            eng.dma_start(weight_rows[:, :, :], weight.rearrange("(t p) c -> p t c", p=P))\
                .then_inc(weight_loaded, 16)
            eng.dma_start(first_x[:, :, :], x_v[0]).then_inc(x_loaded[0], 16)
            for q in range(CHUNKS):
                load_dec(q)
                if q == 0:
                    eng.wait_ge(zeroed, 2)
                    for g in range(4):
                        eng.dma_start(v_raw[g * GR:g * GR + K, :], v_mat).then_inc(v_loaded, 16)
                    for g in range(3):
                        eng.dma_start(bdec_last[g * GR:g * GR + K, :],
                                      b_dec[C * K:(C + 1) * K].rearrange("(k a) -> k a", a=1))\
                            .then_inc(bdec_last_loaded, 16)
                if q == CHUNKS // 2:
                    eng.wait_ge(setup_dve, 12)
                    eng.dma_start(d_dram, d_rows[:, :]).then_inc(d_stored, 16)
            eng.dma_start(bdec_col[:, :, :], b_dec[0:C * K].rearrange("(t p k) -> p t k", p=P, k=K))\
                .then_inc(bdec_loaded, 16)
            eng.dma_start(x_in[1][:, :, :], x_v[1]).then_inc(x_loaded[1], 16)
            eng.wait_ge(d_stored, 16)
            eng.dma_start(d_all[0][:, :], d_dram[0].partition_broadcast(P)).then_inc(d_loaded[0], 16)
            eng.dma_start(bias_all[:, :], bias.partition_broadcast(P)).then_inc(bias_loaded, 16)
            eng.dma_start(d_all[1][:, :], d_dram[1].partition_broadcast(P)).then_inc(d_loaded[1], 16)
            eng.wait_ge(setup_pe, 3 + CT)
            eng.dma_start(x_in[0][:, :, :], x_v[2]).then_inc(x_loaded[0], 16)

            def step(turn, half, seen, last=False):
                b = 2 * turn + half
                if not (isinstance(turn, int) and turn == B // 2 - 1):
                    if seen >= 1:
                        eng.wait_ge(x1_made, NT * (b + 1))
                        eng.dma_start(x_in[half][:, :, :], x_v[b + 2]).then_inc(x_loaded[half], 16)
                    eng.wait_ge(y_scaled, NT * (b + 1))
                    if seen == 0:
                        eng.wait_ge(setup_dve, 16)
                    eng.dma_start(d_all[half][:, :], d_dram[b + 2].partition_broadcast(P))\
                        .then_inc(d_loaded[half], 16)
                if not last:
                    eng.wait_ge(out_ready, NT * (b + 1))
                    eng.dma_start(out_v[b], x1[half][:, :, :]).then_inc(out_stored[half], 16)
                else:
                    for t in range(NT - 2):
                        eng.wait_ge(out_ready, NT * b + t + 1)
                        eng.dma_start(out_v[b][:, t, :], x1[half][:, t, :]).then_inc(out_stored[half], 16)
                    for n, cols in enumerate(HALVES):
                        eng.wait_ge(last_step, HALF_STEPS * (n + 1))
                        eng.dma_start(out_v[b][:, NT - 1, cols], x1[half][:, NT - 1, cols])\
                            .then_inc(out_stored[half], 16)
                        if n == 0:
                            eng.wait_ge(out_ready, NT * B - 1)
                            eng.dma_start(out_v[b][:, NT - 2, :], x1[half][:, NT - 2, :])\
                                .then_inc(out_stored[half], 16)

            step(0, 0, seen=0)
            step(0, 1, seen=1)
            run_steps(eng, step)
            eng.wait_ge(out_stored[0], 16 * (B // 2))
            eng.wait_ge(out_stored[1], 16 * (B // 2 - 1 + NT - 1 + len(HALVES)))

        @block.scalar
        def _(eng):
            eng.dma_start(affb_rows[:, :], affine_b.rearrange("(t p) -> t p", p=P)).then_inc(affb_loaded, 16)
            eng.dma_start(dec_last[:, :, :], dec_v[:, :, C * K:(C + 1) * K]).then_inc(last_loaded, 16)

            eng.wait_ge(zeroed, 3)
            eng.wait_ge(setup_pe, 1)
            eng.activation(cond_t[:, :, 0:B], h_ps[:, 0:MT * B].rearrange("p (m b) -> p m b", m=MT),
                           ACT.Identity)
            eng.activation(affb_col[:, :], h_ps[:, MT * B:MT * B + CT], ACT.Identity)\
                .then_inc(setup_act, 1)
            for m in range(MT):
                eng.wait_ge(setup_pe, 2 + m)
                eng.activation(affine_t[:, m, :], y_ps[m][:, :], ACT.Identity).then_inc(setup_act, 1)
            for c in range(CT):
                eng.wait_ge(setup_pe, 4 + c)
                eng.activation(w_hi[:, c, :], xt_ps[:, c, :], ACT.Identity).then_inc(setup_act, 1)
            for c in range(CT):
                eng.wait_ge(setup_dve, 1 + c)
                eng.activation(w_sq[:, c, :], xt_ps[:, c, :], ACT.Square).then_inc(setup_act, 1)

            def split_xt(turn, half, tiles=range(CT), hi=xt_hi):
                b = 2 * turn + half
                for c in tiles:
                    eng.wait_ge(xt_done, CT * b + c + 1)
                    eng.activation(hi[:, c, :], xt_ps[:, c, :], ACT.Identity).then_inc(xt_hi_done, 1)

            def stack_h(turn, half, nth=None, stack=h_stack[:, :], bank=h_ps):
                nth = 2 * turn + half if nth is None else nth
                eng.wait_ge(tab_ready, nth + 1)
                eng.wait_ge(h_done, nth + 1)
                eng.activation(stack, bank[:, :], ACT.Identity, bias=tab[half][:, U0:U0 + 1])\
                    .then_inc(h_hi_done, 1)

            def split_x1(turn, half, tiles=range(CT)):
                b = 2 * turn + half
                for c in tiles:
                    eng.wait_ge(x1_done, CT * (b - 1) + c + 1)
                    eng.activation(xm_hi[half][:, c, :], xt_ps[:, c, :], ACT.Identity,
                                   scale=tab[half][:, S0 + c:S0 + c + 1]).then_inc(xm_hi_done, 1)

            def prepare(turn, half):
                b = 2 * turn + half
                eng.activation(u_stat[half][:, :, 0:3, :],
                               u_all[:, b, :, :].unsqueeze(2).broadcast_to([P, CT, 3, GR]), ACT.Identity)\
                    .then_inc(u_hi_done, 1)
                eng.activation(tab[half][:, :], tab_all[:, b, :], ACT.Identity).then_inc(tab_ready, 1)

            def keep_rows(q):
                eng.wait_ge(u_made, q + 1)
                eng.activation(u_rows[:, CHUNK_ENDS[q]:CHUNK_ENDS[q + 1]],
                               y_ps[q % 2][:, 0:CHUNK_ENDS[q + 1] - CHUNK_ENDS[q]], ACT.Identity)\
                    .then_inc(u_in_rows, 1)

            def keep_first_y(t):
                eng.wait_ge(y_done, t + 1)
                eng.activation(y[:, t, :], xt_ps[:, t, :], ACT.Identity).then_inc(first_y_kept, 1)

            split_xt(0, 0)
            for c in range(CT):
                eng.wait_ge(xt_lo_done, c + 1)
                eng.activation(xm_hi[0][:, c, :], xt_ps[:, c, :], ACT.Identity,
                               scale=tab_all[:, 0, S0 + c:S0 + c + 1]).then_inc(xm_hi_done, 1)
            eng.wait_ge(setup_dve, 7)
            eng.activation(inv[:, :], var[:, :], ACT.Sqrt).then_inc(setup_act, 1)
            keep_rows(0)
            eng.wait_ge(v_loaded, 16 * 4)
            eng.activation(v_stat[:, :], v_raw[:, :], ACT.Identity).then_inc(setup_act, 1)
            keep_rows(1)
            keep_first_y(0)
            eng.wait_ge(setup_pe, 11)
            for c in range(CT):
                last = eng.activation(vt_hi[:, c, :], r_ps[:, c * P:(c + 1) * P], ACT.Identity,
                                      scale=tab_all[:, 0, S0 + c:S0 + c + 1])
            last.then_inc(setup_act, 1)
            keep_rows(2)
            keep_first_y(1)
            keep_rows(3)
            keep_first_y(2)
            keep_rows(4)
            keep_rows(5)
            keep_first_y(3)
            for q in range(6, CHUNKS):
                keep_rows(q)
            split_xt(0, 1, range(2), early_hi)
            eng.wait_ge(u_kept, U_BANKS)
            prepare(0, 1)
            split_xt(0, 1, range(2, CT), early_hi)
            prepare(0, 0)
            stack_h(0, 1, 0, bank=r_ps)
            eng.wait_ge(setup_dve, 16)
            eng.activation(va_stat[:, :], va_rows, ACT.Identity).then_inc(setup_act, 1)
            split_x1(0, 1, range(1))
            stack_h(0, 0, 1, first_h, y_ps[1])
            split_x1(0, 1, range(1, 3))
            for t in range(NT):
                eng.wait_ge(rank_done, t + 1)
                eng.activation(first_rank[:, t, :], rank_ps[t % 2][:, :], ACT.Identity).then_inc(first_rank_kept, 1)
                if t == 0:
                    split_x1(0, 1, range(3, CT))
            eng.wait_ge(h_stacked, 2)
            prepare(1, 0)

            def step(turn, half, seen, last=False):
                nxt = (turn + half, 1 - half)
                if last:
                    return
                split_xt(*nxt)
                stack_h(*nxt)
                split_x1(*nxt)
                if not (isinstance(turn, int) and turn == B // 2 - 1):
                    prepare(turn + 1, half)

            step(0, 1, seen=1)
            run_steps(eng, step)

        @block.vector
        def _(eng):
            for c in range(CT):
                eng.wait_ge(setup_act, 4 + c)
                eng.tensor_tensor(w_lo[:, c, :], xt_ps[:, c, :], w_hi[:, c, :].bitcast(fp32),
                                  ALU.subtract).then_inc(setup_dve, 1)
            eng.wait_ge(setup_act, 1)
            eng.wait_ge(setup_pe, 4 + CT)
            s_view = tab_all[:, :, S0:S0 + CT].rearrange("p b c -> p c b")
            eng.scalar_tensor_tensor(s_view, r_ps[:, 0:CT * B].rearrange("p (c b) -> p c b", c=CT), GAIN,
                                     affb_col[:, :].unsqueeze(2).broadcast_to([P, CT, B]),
                                     ALU.mult, ALU.add).then_inc(setup_dve, 1)
            eng.wait_ge(setup_dve, 5)
            eng.tensor_tensor(style_sq[:, :, :], s_view, s_view, ALU.mult).then_inc(setup_dve, 1)

            def split_xt(turn, half, tiles=range(CT), hi=xt_hi, lo=xt_lo):
                b = 2 * turn + half
                for c in tiles:
                    eng.wait_ge(xt_hi_done, CT * b + c + 1)
                    eng.tensor_tensor(lo[:, c, :], xt_ps[:, c, :], hi[:, c, :].bitcast(fp32),
                                      ALU.subtract).then_inc(xt_lo_done, 1)

            def stack_h(turn, half, nth=None, stack=h_stack, bank=h_ps):
                nth = 2 * turn + half if nth is None else nth
                lo = slice(2 * GR, 3 * GR)
                eng.wait_ge(h_hi_done, nth + 1)
                eng.scalar_tensor_tensor(stack[lo, :], bank[lo, :], tab[half][lo, U0:U0 + 1],
                                         stack[lo, :].bitcast(fp32), ALU.add, ALU.subtract)\
                    .then_inc(h_stacked, 1)

            def split_x1(turn, half, tiles=range(CT)):
                b = 2 * turn + half
                for c in tiles:
                    eng.wait_ge(xm_hi_done, CT * b + c + 1)
                    eng.scalar_tensor_tensor(xm_lo[half][:, c, :], xt_ps[:, c, :], tab[half][:, S0 + c:S0 + c + 1],
                                             xm_hi[half][:, c, :].bitcast(fp32), ALU.mult, ALU.subtract)\
                        .then_inc(xm_lo_done, 1)

            def u_low(turn, half, nth=None):
                b = 2 * turn + half
                nth = b if nth is None else nth
                eng.wait_ge(u_hi_done, nth + 1)
                eng.tensor_tensor(u_stat[half][:, :, 3, :], u_all[:, b, :, :], u_stat[half][:, :, 0, :].bitcast(fp32),
                                  ALU.subtract).then_inc(u_stat_ready, 1)

            def make_x1(turn, half, t, seen):
                b = 2 * turn + half
                if t == 0 and seen >= 2:
                    eng.wait_ge(out_stored[half], 16 * turn)
                eng.wait_ge(rank_done, NT * b + t + 1)
                eng.tensor_tensor(x1[half][:, t, :], rank_ps[t % 2][:, :], x_in[half][:, t, :], ALU.add)\
                    .then_inc(x1_made, 1)

            def scale_y(turn, half, t, seen):
                n = NT * (2 * turn + half) + t
                if t == 0:
                    eng.wait_ge(d_loaded[half], 16 * (turn + 1))
                if seen >= 1:
                    eng.wait_ge(out_ready, n - NT + 1)
                eng.wait_ge(y_done, n + 1)
                eng.tensor_tensor(y[:, t, :], y_ps[t % 2][:, :], d_all[half][:, :], ALU.mult)\
                    .then_inc(y_scaled, 1)

            def clip(turn, half, t):
                eng.wait_ge(biased, NT * (2 * turn + half) + t + 1)
                eng.tensor_scalar(y[:, t, :], y[:, t, :], CLAMP, -CLAMP, ALU.min, ALU.max).then_inc(clipped, 1)

            split_xt(0, 0)
            for c in range(CT):
                eng.wait_ge(xm_hi_done, c + 1)
                eng.scalar_tensor_tensor(xm_lo[0][:, c, :], xt_ps[:, c, :], tab_all[:, 0, S0 + c:S0 + c + 1],
                                         xm_hi[0][:, c, :].bitcast(fp32), ALU.mult, ALU.subtract)\
                    .then_inc(xm_lo_done, 1)
            eng.wait_ge(setup_pe, 9)
            eng.tensor_scalar(var[:, :], r_ps[0:B, :], EPS, None, ALU.add).then_inc(setup_dve, 1)
            eng.wait_ge(setup_act, 12)
            eng.reciprocal(inv[:, :], inv[:, :]).then_inc(setup_dve, 1)
            eng.wait_ge(setup_dve, 8)
            eng.tensor_tensor(newton[:, :], inv[:, :], inv[:, :], ALU.mult).then_inc(setup_dve, 1)
            eng.wait_ge(setup_dve, 9)
            eng.tensor_tensor(newton[:, :], newton[:, :], var[:, :], ALU.mult).then_inc(setup_dve, 1)
            eng.wait_ge(setup_dve, 10)
            eng.tensor_scalar(newton[:, :], newton[:, :], -0.5, 1.5, ALU.mult, ALU.add)\
                .then_inc(setup_dve, 1)
            eng.wait_ge(setup_dve, 11)
            eng.tensor_tensor(d_rows[:, :], inv[:, :], newton[:, :], ALU.mult).then_inc(setup_dve, 1)
            eng.wait_ge(setup_pe, 10)
            eng.wait_ge(bdec_last_loaded, 16 * 3)
            eng.tensor_scalar(tab_all[:, :, U0:U0 + 1], h_ps[:, 0:B].unsqueeze(2), bdec_last[:, 0:1], None,
                              ALU.add).then_inc(setup_dve, 1)
            group1 = slice(GR, 2 * GR)
            eng.wait_ge(setup_act, 13)
            eng.tensor_tensor(v_stat[group1, :], v_raw[group1, :], v_stat[group1, :].bitcast(fp32),
                              ALU.subtract).then_inc(setup_dve, 1)
            eng.wait_ge(setup_act, 14)
            for c in range(CT):
                last = eng.scalar_tensor_tensor(vt_lo[:, c, :], r_ps[:, c * P:(c + 1) * P],
                                                tab_all[:, 0, S0 + c:S0 + c + 1], vt_hi[:, c, :].bitcast(fp32),
                                                ALU.mult, ALU.subtract)
            last.then_inc(setup_dve, 1)
            eng.wait_ge(zeroed, 4)
            eng.wait_ge(bdec_loaded, 16)
            for n, k0 in enumerate(range(0, K, KB)):
                ranks = min(KB, K - k0)
                eng.wait_ge(u_turned, n + 1)
                eng.tensor_tensor(
                    u_all[:, :, :, k0:k0 + ranks].rearrange("p b t k -> p k t b"),
                    turn_ps[n % 3][:, 0:ranks * P].rearrange("p (k t b) -> p k t b", k=ranks, t=CT)[:, :, :, 0:B],
                    bdec_col[:, :, k0:k0 + ranks].rearrange("p t k -> p k t").unsqueeze(3)
                    .broadcast_to([P, ranks, CT, B]), ALU.add).then_inc(u_kept, 1)
                if n == 4:
                    split_xt(0, 1, range(1), early_hi, early_lo)
            split_xt(0, 1, range(1, 2), early_hi, early_lo)
            u_low(0, 1, 0)
            split_xt(0, 1, range(2, CT), early_hi, early_lo)
            u_low(0, 0, 1)
            eng.wait_ge(setup_pe, 12)
            eng.wait_ge(d_loaded[0], 16)
            eng.tensor_tensor(va_rows, h_ps[:, :], d_all[0][:, :], ALU.mult).then_inc(setup_dve, 1)
            stack_h(0, 1, 0, bank=r_ps)
            eng.wait_ge(setup_act, 15)
            eng.tensor_tensor(va_stat[group1, :], va_rows[group1, :], va_stat[group1, :].bitcast(fp32),
                              ALU.subtract).then_inc(setup_dve, 1)
            split_x1(0, 1, range(1))
            stack_h(0, 0, 1, first_h, y_ps[1])
            split_x1(0, 1, range(1, CT))

            def add_first(t):
                eng.wait_ge(biased, t + 1)
                eng.wait_ge(first_y_done, t + 1)
                eng.tensor_tensor(y[:, t, :], y[:, t, :], xt_ps[:, t, :], ALU.add).then_inc(first_y_added, 1)

            def clip_first(t):
                eng.wait_ge(first_y_added, t + 1)
                clip(0, 0, t)

            add_first(0)
            clip_first(0)
            for t in range(1, NT):
                add_first(t)
            for t in range(1, NT):
                clip_first(t)
            eng.wait_ge(x1_made, NT)
            make_x1(0, 1, 0, 1)
            make_x1(0, 1, 1, 1)
            scale_y(0, 1, 0, 1)
            split_xt(1, 0)
            make_x1(0, 1, 2, 1)
            make_x1(0, 1, 3, 1)
            u_low(1, 0)
            scale_y(0, 1, 1, 1)
            clip(0, 1, 0)
            stack_h(1, 0)
            scale_y(0, 1, 2, 1)
            clip(0, 1, 1)
            split_x1(1, 0, range(CT - 1))
            make_x1(1, 0, 0, 2)
            split_x1(1, 0, range(CT - 1, CT))
            make_x1(1, 0, 1, 2)
            clip(0, 1, 2)
            scale_y(0, 1, 3, 1)
            u_low(1, 1)

            def step(turn, half, seen, last=False):
                nxt, prev = (turn + half, 1 - half), (turn + half - 1, 1 - half)
                make_x1(turn, half, 2, seen)
                make_x1(turn, half, 3, seen)
                if seen >= 1:
                    clip(*prev, 3)
                scale_y(turn, half, 0, seen)
                if not last:
                    split_xt(*nxt)
                clip(turn, half, 0)
                scale_y(turn, half, 1, seen)
                if not last:
                    stack_h(*nxt)
                clip(turn, half, 1)
                scale_y(turn, half, 2, seen)
                if not last:
                    split_x1(*nxt)
                    make_x1(*nxt, 0, seen + 1)
                    make_x1(*nxt, 1, seen + 1)
                    clip(turn, half, 2)
                    scale_y(turn, half, 3, seen)
                if not (isinstance(turn, int) and turn == B // 2 - 1):
                    u_low(turn + 1, half)
                if last:
                    t = NT - 1
                    eng.wait_ge(out_ready, NT * (B - 1))
                    for n, cols in enumerate(HALVES):
                        eng.wait_ge(last_y_done, n + 1)
                        eng.tensor_tensor(y[:, t, cols], last_ps[n][:, cols], d_all[half][:, cols], ALU.mult)\
                            .then_inc(last_step, 1)
                        eng.wait_ge(last_step, HALF_STEPS * n + 1)
                        eng.tensor_tensor(y[:, t, cols], y[:, t, cols], bias_all[:, cols], ALU.add)\
                            .then_inc(last_step, 1)
                        eng.wait_ge(last_step, HALF_STEPS * n + 2)
                        eng.tensor_scalar(y[:, t, cols], y[:, t, cols], CLAMP, -CLAMP, ALU.min, ALU.max)\
                            .then_inc(last_step, 1)
                        eng.wait_ge(last_step, HALF_STEPS * n + 3)
                        eng.tensor_tensor(x1[half][:, t, cols], x1[half][:, t, cols], y[:, t, cols], ALU.add)\
                            .then_inc(last_step, 1)
                        if n == 0:
                            clip(turn, half, NT - 2)

            run_steps(eng, step)

        @block.gpsimd
        def _(eng):
            eng.memset(v_raw[:, :], 0.0).then_inc(zeroed, 1)
            eng.memset(bdec_last[:, :], 0.0).then_inc(zeroed, 1)
            eng.memset(cond_t[:, :, :], 0.0).then_inc(zeroed, 1)
            eng.memset(ident[:, :], 0.0).then_inc(ident_ready, 1)
            eng.wait_ge(ident_ready, 1)
            eng.affine_select(out=ident[:, :], in_=ident[:, :], compare_op=ALU.not_equal, fill=1.0,
                              base=0, pattern=[[-1, P]], channel_multiplier=1).then_inc(ident_ready, 1)
            eng.memset(u_all[:, :, :, :], 0.0).then_inc(zeroed, 1)
            eng.memset(dec_last4[:, :, :, :], 0.0).then_inc(last_ready, 1)
            eng.wait_ge(last_ready, 1)
            eng.wait_ge(last_loaded, 16)
            eng.tensor_copy(dec_last4[:, :, 0:3, 0:K],
                            dec_last[:, :, :].unsqueeze(2).broadcast_to([P, MT, 3, K])).then_inc(last_ready, 1)

            def add_bias(turn, half, t):
                eng.wait_ge(y_scaled, NT * (2 * turn + half) + t + 1)
                eng.tensor_tensor(y[:, t, :], y[:, t, :], bias_all[:, :], ALU.add).then_inc(biased, 1)

            def finish(turn, half, t):
                b = 2 * turn + half
                eng.wait_ge(x1_made, NT * b + t + 1)
                eng.wait_ge(clipped, NT * b + t + 1)
                eng.tensor_tensor(x1[half][:, t, :], x1[half][:, t, :], y[:, t, :], ALU.add).then_inc(out_ready, 1)

            def step(turn, half, seen, last=False):
                add_bias(turn, half, 0)
                if seen >= 2:
                    finish(turn + half - 1, 1 - half, 3)
                for t in range(1, NT):
                    if not (last and t == NT - 1):
                        add_bias(turn, half, t)
                    finish(turn, half, t - 1)

            eng.wait_ge(d_loaded[0], 16)
            for t in range(NT):
                eng.wait_ge(first_y_kept, t + 1)
                eng.tensor_tensor(y[:, t, :], y[:, t, :], d_all[0][:, :], ALU.mult).then_inc(y_scaled, 1)
            eng.wait_ge(bias_loaded, 16)
            for t in range(NT):
                add_bias(0, 0, t)

            def first_x1(t):
                eng.wait_ge(first_rank_kept, t + 1)
                eng.tensor_tensor(x1[0][:, t, :], first_x[:, t, :], first_rank[:, t, :], ALU.add).then_inc(x1_made, 1)

            for t in range(NT):
                first_x1(t)
            for t in range(NT):
                finish(0, 0, t)
            step(0, 1, seen=1)
            run_steps(eng, step)

        @block.tensor
        def _(eng):
            eng.wait_ge(ident_ready, 2)
            eng.wait_ge(cond_loaded, 16)
            for m in range(MT):
                eng.transpose(h_ps[:, m * B:(m + 1) * B], cond_rows[:, m * P:(m + 1) * P], ident[0:B, 0:B])
            eng.wait_ge(affb_loaded, 16)
            eng.transpose(h_ps[:, MT * B:MT * B + CT], affb_rows[:, :], ident[0:CT, 0:CT])\
                .then_inc(setup_pe, 1)

            def make_u(q):
                cols = CHUNK_ENDS[q + 1] - CHUNK_ENDS[q]
                for m in range(MT):
                    eng.wait_ge(dec_loaded[q % DEC_BUFS][m], 16 * (q // DEC_BUFS + 1))
                    for t in range(CT):
                        last = eng.matmul(y_ps[q % 2][t * BG:(t + 1) * BG, 0:cols], cond_t[:, m, :],
                                          dec[q % DEC_BUFS][:, m, t, 0:cols], start=m == 0, stop=m == MT - 1,
                                          tile_position=(0, t * BG))
                last.then_inc(u_made, 1)

            eng.wait_ge(affine_loaded, 16)
            for m in range(MT):
                for c in range(CT):
                    last = eng.transpose(y_ps[m][:, c * P:(c + 1) * P], affine_rows[:, c, m * P:(m + 1) * P],
                                         ident[:, :])
                last.then_inc(setup_pe, 1)
            eng.wait_ge(weight_loaded, 16)
            for c in range(CT):
                for o in range(CT):
                    last = eng.transpose(xt_ps[:, c, o * P:(o + 1) * P], weight_rows[:, o, c * P:(c + 1) * P],
                                         ident[:, :])
                last.then_inc(setup_pe, 1)
            eng.wait_ge(setup_act, 3)
            for c in range(CT):
                for m in range(MT):
                    last = eng.matmul(r_ps[:, c * B:(c + 1) * B], affine_t[:, m, c * P:(c + 1) * P],
                                      cond_t[:, m, 0:B], start=m == 0, stop=m == MT - 1)
            last.then_inc(setup_pe, 1)

            def transpose_x(turn, half, source=None, tiles=range(CT), first_y=False):
                eng.wait_ge(x_loaded[half], 16 * (turn + 1))
                for c in tiles:
                    if first_y:
                        eng.wait_ge(first_y_added, c + 1)
                    for t in range(TT):
                        last = eng.matmul(xt_ps[:, c, t * P:(t + 1) * P],
                                          (source or x_in[half])[:, t, c * P:(c + 1) * P],
                                          ident[:, :], is_transpose=True, start=t == 0, stop=False,
                                          skip_group_check=True)
                    last.then_inc(xt_done, 1)

            def product_h(turn, half, seen, nth=None, parts=(xt_hi, xt_lo), bank=h_ps):
                b = 2 * turn + half
                eng.wait_ge(u_stat_ready, (b if nth is None else nth) + 1)
                if seen >= 1:
                    eng.wait_ge(x1_made, NT * b)
                for c in range(CT):
                    u_c = u_stat[half][:, c, :, :].rearrange("p g k -> p (g k)")
                    for part, parted in enumerate((xt_hi_done, xt_lo_done)):
                        eng.wait_ge(parted, CT * b + c + 1)
                        last = eng.matmul(bank[:, :], u_c, parts[part][:, c, :], start=c == 0 and part == 0,
                                          stop=c == CT - 1 and part == 1)
                last.then_inc(h_done, 1)

            def add_rank(turn, half, nth=None):
                b = 2 * turn + half
                eng.wait_ge(h_stacked, (b if nth is None else nth) + 1)
                for c in range(CT):
                    eng.matmul(xt_ps[:, c, :], v_stat[:, c * P:(c + 1) * P], h_stack[:, :], start=False,
                               stop=True, skip_group_check=True).then_inc(x1_done, 1)

            def rank_tile(turn, half, t, stack=h_stack[:, :], freed=False):
                b = 2 * turn + half
                if t >= 2 and not freed:
                    eng.wait_ge(x1_made, NT * b + t - 1)
                eng.matmul(rank_ps[t % 2][:, :], stack[:, t * P:(t + 1) * P], v_stat[:, :], start=True, stop=True)\
                    .then_inc(rank_done, 1)

            def main_tile(turn, half, t, seen, between=None, bank=None):
                b = 2 * turn + half
                n = NT * b + t
                if seen >= 1:
                    eng.wait_ge(y_scaled, n - 1)
                toks = slice(t * P, (t + 1) * P)
                bank = bank or y_ps[t % 2][:, :]
                for c in range(CT):
                    if t == 0:
                        eng.wait_ge(xm_lo_done, CT * b + c + 1)
                    eng.matmul(bank, xm_hi[half][:, c, toks], w_hi[:, c, :], start=c == 0, stop=False)
                    eng.matmul(bank, xm_hi[half][:, c, toks], w_lo[:, c, :], start=False, stop=False)
                    last = eng.matmul(bank, xm_lo[half][:, c, toks], w_hi[:, c, :], start=False,
                                      stop=c == CT - 1)
                    if between and c < CT - 1:
                        between(c)
                last.then_inc(y_done, 1)
                if between:
                    between(CT - 1)

            make_u(0)
            eng.wait_ge(setup_act, 11)
            transpose_x(0, 0, first_x)
            eng.wait_ge(setup_dve, 6)
            for c in range(CT):
                last = eng.matmul(r_ps[0:B, :], style_sq[:, c, :], w_sq[:, c, :], start=c == 0, stop=c == CT - 1)
            last.then_inc(setup_pe, 1)
            eng.wait_ge(last_ready, 2)
            for m in range(MT):
                last = eng.matmul(h_ps[:, 0:B], dec_last4[:, m, :, :].rearrange("p g k -> p (g k)"),
                                  cond_t[:, m, 0:B], start=m == 0, stop=m == MT - 1)
            last.then_inc(setup_pe, 1)
            make_u(1)
            eng.wait_ge(xm_lo_done, CT)
            main_tile(0, 0, 0, 0, bank=xt_ps[:, 0, :])
            eng.wait_ge(u_in_rows, 1)
            make_u(2)
            eng.wait_ge(v_loaded, 16 * 4)
            eng.wait_ge(setup_dve, 7)
            for c in range(CT):
                last = eng.transpose(r_ps[:, c * P:(c + 1) * P], v_raw[:, c * P:(c + 1) * P], ident[:, :])
            last.then_inc(setup_pe, 1)
            main_tile(0, 0, 1, 0, bank=xt_ps[:, 1, :])
            eng.wait_ge(u_in_rows, 2)
            make_u(3)
            main_tile(0, 0, 2, 0, bank=xt_ps[:, 2, :])
            eng.wait_ge(u_in_rows, 3)
            make_u(4)
            eng.wait_ge(setup_dve, 15)
            for c in range(CT):
                eng.matmul(h_ps[:, :], vt_hi[:, c, :], w_hi[:, c, :], start=c == 0, stop=False)
                eng.matmul(h_ps[:, :], vt_hi[:, c, :], w_lo[:, c, :], start=False, stop=False)
                last = eng.matmul(h_ps[:, :], vt_lo[:, c, :], w_hi[:, c, :], start=False, stop=c == CT - 1)
            last.then_inc(setup_pe, 1)
            eng.wait_ge(u_in_rows, 4)
            make_u(5)
            main_tile(0, 0, 3, 0, bank=xt_ps[:, 3, :])
            eng.wait_ge(u_in_rows, 5)
            make_u(6)
            eng.wait_ge(u_in_rows, 6)
            make_u(CHUNKS - 1)
            eng.wait_ge(u_in_rows, CHUNKS)
            for n, k0 in enumerate(range(0, K, KB)):
                if n >= 3:
                    eng.wait_ge(u_kept, n - 2)
                for k in range(k0, min(k0 + KB, K)):
                    last = eng.transpose(turn_ps[n % 3][:, (k - k0) * P:(k - k0 + 1) * P],
                                         u_rows[:, k:k + (P - 1) * K + 1:K], ident[:, :])
                last.then_inc(u_turned, 1)
                if n == 4:
                    eng.wait_ge(first_y_kept, NT)
                    transpose_x(0, 1, tiles=range(2))
            transpose_x(0, 1, tiles=range(2, CT))
            eng.wait_ge(u_kept, U_BANKS)
            product_h(0, 1, 0, 0, (early_hi, early_lo), bank=r_ps)
            product_h(0, 0, 0, 1, bank=y_ps[1])
            add_rank(0, 1, 0)

            def first_in_tile_0(c):
                if c == 0:
                    eng.wait_ge(h_stacked, 2)
                    rank_tile(0, 0, 0, first_h)
                    rank_tile(0, 0, 1, first_h)
                eng.matmul(xt_ps[:, c, :], first_h[:, c * P:(c + 1) * P], va_stat[:, :], start=True, stop=True)\
                    .then_inc(first_y_done, 1)
                if c >= 2:
                    eng.wait_ge(first_rank_kept, c - 1)
                    rank_tile(0, 0, c, first_h, freed=True)

            def more_in_tile_1(c):
                if c < 2:
                    eng.wait_ge(first_rank_kept, c + 3)
                    rank_tile(0, 1, c)
                if c == 1:
                    transpose_x(1, 0, first_y=True)

            def ranks_in_tile_2(c):
                if c < 2:
                    rank_tile(0, 1, c + 2)

            def next_in_tile_3(c):
                if c == 2:
                    add_rank(1, 0)
                elif c == 3:
                    rank_tile(1, 0, 0)
                    rank_tile(1, 0, 1)

            main_tile(0, 1, 0, 1, between=first_in_tile_0)
            main_tile(0, 1, 1, 1, between=more_in_tile_1)
            main_tile(0, 1, 2, 1, between=ranks_in_tile_2)
            product_h(1, 0, 2)
            main_tile(0, 1, 3, 1, between=next_in_tile_3)

            def step(turn, half, seen, last=False):
                nxt = (turn + half, 1 - half)
                main_tile(turn, half, 0, seen,
                          between=lambda c: rank_tile(turn, half, c) if c >= 2 else None)
                if not last:
                    transpose_x(*nxt)
                main_tile(turn, half, 1, seen)
                if not last:
                    product_h(*nxt, seen + 1)
                main_tile(turn, half, 2, seen)
                if not last:
                    add_rank(*nxt)
                    rank_tile(*nxt, 0)
                    rank_tile(*nxt, 1)
                    main_tile(turn, half, 3, seen)
                    return
                eng.wait_ge(x1_made, NT * B - 1)
                eng.wait_ge(y_scaled, NT * B - 2)
                toks = slice((NT - 1) * P, NT * P)
                for cols, bank in zip(HALVES, last_ps):
                    for c in range(CT):
                        eng.matmul(bank[:, cols], xm_hi[half][:, c, toks], w_hi[:, c, cols], start=c == 0, stop=False)
                        eng.matmul(bank[:, cols], xm_hi[half][:, c, toks], w_lo[:, c, cols], start=False, stop=False)
                        done = eng.matmul(bank[:, cols], xm_lo[half][:, c, toks], w_hi[:, c, cols], start=False,
                                          stop=c == CT - 1)
                    done.then_inc(last_y_done, 1)

            run_steps(eng, step)


_INS = ["x", "cond_512", "L0_cond_W_dec", "L0_cond_b_dec", "L0_cond_V", "L1_cond_weight", "L1_cond_bias",
        "L1_cond_affine_w", "L1_cond_affine_b"]


def kernel(**inputs):
    import numpy as _np
    import concourse.bacc as _bacc
    from concourse import mybir as _mybir
    from concourse.bass_utils import run_bass_kernel_spmd as _run

    nc = _bacc.Bacc("TRN2", target_bir_lowering=False, num_devices=1)
    arrays, args = {}, []
    for name in _INS:
        a = _np.ascontiguousarray(inputs[name])
        arrays[f"in_{name}_dram"] = a
        args.append(nc.dram_tensor(f"in_{name}_dram", a.shape, _mybir.dt.from_np(a.dtype), kind="ExternalInput").ap())
    shape = tuple(inputs["x"].shape)
    args.append(nc.dram_tensor("out_0_dram", shape, _mybir.dt.float32, kind="ExternalOutput").ap())
    build(nc, *args)
    r = _run(nc, [arrays], core_ids=[0])
    return r.results[0]["out_0_dram"]
```
